# Optimizing a Trainium2 kernel written in Bass

```python
import numpy as np
import jax
import jax.numpy as jnp

def _softmax(x, axis=-1):
    return jax.nn.softmax(x, axis=axis)
def _gelu(x):
    return jax.nn.gelu(x, approximate=True)
def _silu(x):
    return jax.nn.silu(x)
def _sigmoid(x):
    return jax.nn.sigmoid(x)
def _layernorm(x, axis=-1, eps=1e-5):
    m = jnp.mean(x, axis=axis, keepdims=True)
    v = jnp.var(x, axis=axis, keepdims=True)
    return (x - m) / jnp.sqrt(v + eps)
def _scatter_add(tgt, idx, src, axis=0):
    return tgt.at[idx].add(src)
def _segment_sum(src, seg, n):
    return jax.ops.segment_sum(src, seg, n)

kernel_name = 'mk_adj_preln_d2_adj_256_10ca76'

def setup_inputs(seed: int = 0):
    np.random.seed(seed)
    _w = jnp.asarray
    def _rec_inputs():
        import jax
        import jax.numpy as jnp
        _gk = jax.random.key(seed)
        x = -0.0005207 + 1.001 * jax.random.normal(jax.random.fold_in(_gk, 1), (8, 2048, 256), jnp.float32)
        _a = jax.random.bernoulli(jax.random.fold_in(_gk, 2), 0.00195312, (2048, 2048))
        _a = jnp.logical_or(_a, jnp.swapaxes(_a, -1, -2))
        _a = jnp.logical_or(_a, jnp.eye(2048, dtype=bool))
        adj = _a.astype(jnp.int32)
        return x, adj
    x, adj = _rec_inputs()
    def _L0_gnn_setup():
        import jax, jax.numpy as jnp
        import numpy as np
        import math
        CHUNK = 256
        NUM_HEADS = 4
        EPS = 1e-05
        key = jax.random.key(seed)
        ks = jax.random.split(key, 12)
        B, N, F = (4, 2048, 256)
        x = jax.random.normal(ks[0], (B, N, F), dtype=jnp.float32)
        adj_matrix = jax.random.randint(ks[1], (N, N), 0, 2, dtype=jnp.int32)
        s = 1.0 / math.sqrt(F)
        Wq = jax.random.normal(ks[2], (F, F), dtype=jnp.float32) * s
        bq = jnp.zeros((F,), dtype=jnp.float32)
        Wk = jax.random.normal(ks[3], (F, F), dtype=jnp.float32) * s
        bk = jnp.zeros((F,), dtype=jnp.float32)
        Wv = jax.random.normal(ks[4], (F, F), dtype=jnp.float32) * s
        bv = jnp.zeros((F,), dtype=jnp.float32)
        Wo = jax.random.normal(ks[5], (F, F), dtype=jnp.float32) * s
        bo = jnp.zeros((F,), dtype=jnp.float32)
        gamma = jnp.ones((F,), dtype=jnp.float32)
        beta = jnp.zeros((F,), dtype=jnp.float32)
        return {'x': x, 'adj_matrix': adj_matrix, 'Wq': Wq, 'bq': bq, 'Wk': Wk, 'bk': bk, 'Wv': Wv, 'bv': bv, 'Wo': Wo, 'bo': bo, 'gamma': gamma, 'beta': beta}
    _L0_gnn_all = _L0_gnn_setup()
    _L0_gnn_in = {k: v for k, v in _L0_gnn_all.items() if k in ('Wq', 'bq', 'Wk', 'bk', 'Wv', 'bv', 'Wo', 'bo', 'gamma', 'beta', )}
    del _L0_gnn_all

    def _L1_gnn_setup():
        import jax, jax.numpy as jnp
        import numpy as np
        ALPHA = 0.2
        MASK_VAL = -9000000000000000.0
        key = jax.random.key(seed)
        k1, k2, k3, k4 = jax.random.split(key, 4)
        B, N, F = (8, 1024, 256)
        H, OUT = (4, 256)
        hs = OUT // H
        x = jax.random.normal(k1, (B, N, F), dtype=jnp.float32)
        adj = jax.random.randint(k2, (N, N), 0, 2, dtype=jnp.int32)
        wb = float(np.sqrt(6.0 / (F + hs)))
        ab = float(np.sqrt(6.0 / (H + 2 * hs)))
        W = jax.random.uniform(k3, (H, F, hs), dtype=jnp.float32, minval=-wb, maxval=wb)
        a = jax.random.uniform(k4, (H, 2 * hs), dtype=jnp.float32, minval=-ab, maxval=ab)
        return {'x': x, 'adj': adj, 'W': W, 'a': a}
    _L1_gnn_all = _L1_gnn_setup()
    _L1_gnn_in = {k: v for k, v in _L1_gnn_all.items() if k in ('W', 'a', )}
    del _L1_gnn_all

    return {
        "x": x,
        "adj": adj,
        "L0_gnn_Wq": _L0_gnn_in["Wq"],
        "L0_gnn_bq": _L0_gnn_in["bq"],
        "L0_gnn_Wk": _L0_gnn_in["Wk"],
        "L0_gnn_bk": _L0_gnn_in["bk"],
        "L0_gnn_Wv": _L0_gnn_in["Wv"],
        "L0_gnn_bv": _L0_gnn_in["bv"],
        "L0_gnn_Wo": _L0_gnn_in["Wo"],
        "L0_gnn_bo": _L0_gnn_in["bo"],
        "L0_gnn_gamma": _L0_gnn_in["gamma"],
        "L0_gnn_beta": _L0_gnn_in["beta"],
        "L1_gnn_W": _L1_gnn_in["W"],
        "L1_gnn_a": _L1_gnn_in["a"],
    }

def reference(x, adj, L0_gnn_Wq, L0_gnn_bq, L0_gnn_Wk, L0_gnn_bk, L0_gnn_Wv, L0_gnn_bv, L0_gnn_Wo, L0_gnn_bo, L0_gnn_gamma, L0_gnn_beta, L1_gnn_W, L1_gnn_a):
    import jax
    import jax.numpy as jnp
    def _L0_gnn_ref(x, adj_matrix, Wq, bq, Wk, bk, Wv, bv, Wo, bo, gamma, beta):
        import jax, jax.numpy as jnp
        import numpy as np
        import math
        CHUNK = 256
        NUM_HEADS = 4
        EPS = 1e-05
        B, N, Fin = x.shape
        H = NUM_HEADS
        Dout = Wq.shape[0]
        Dh = Dout // H
        Nc = N // CHUNK
        q = (x @ Wq.T + bq).reshape(B, N, H, Dh).transpose(0, 2, 1, 3)
        k = (x @ Wk.T + bk).reshape(B, N, H, Dh).transpose(0, 2, 1, 3)
        v = (x @ Wv.T + bv).reshape(B, N, H, Dh).transpose(0, 2, 1, 3)
        kc = k.reshape(B, H, Nc, CHUNK, Dh)
        vc = v.reshape(B, H, Nc, CHUNK, Dh)
        scores = jnp.einsum('bhnd,bhjcd->bhnjc', q, kc) / jnp.sqrt(jnp.asarray(Dh, dtype=q.dtype))
        scores = jnp.clip(scores, -10.0, 10.0)
        mask = adj_matrix.reshape(N, Nc, CHUNK)[None, None]
        scores = jnp.where(mask == 0, jnp.asarray(-10.0, scores.dtype), scores)
        attn = jax.nn.softmax(scores, axis=-1)
        ctx = jnp.einsum('bhnjc,bhjcd->bhnd', attn, vc)
        ctx = ctx.transpose(0, 2, 1, 3).reshape(B, N, Dout)
        out = ctx @ Wo.T + bo
        out = out + x
        mu = jnp.mean(out, axis=-1, keepdims=True)
        var = jnp.mean(jnp.square(out - mu), axis=-1, keepdims=True)
        out = (out - mu) * jax.lax.rsqrt(var + EPS) * gamma + beta
        return out

    def _L1_gnn_ref(x, adj, W, a):
        import jax, jax.numpy as jnp
        import numpy as np
        ALPHA = 0.2
        MASK_VAL = -9000000000000000.0
        B, N, _ = x.shape
        H, _, hs = W.shape
        Wh = jnp.einsum('bnf,hfd->bhnd', x, W)
        a1, a2 = (a[:, :hs], a[:, hs:])
        ei = jnp.einsum('bhnd,hd->bhn', Wh, a1)
        ej = jnp.einsum('bhnd,hd->bhn', Wh, a2)
        e = ei[:, :, :, None] + ej[:, :, None, :]
        e = jnp.where(e > 0, e, ALPHA * e)
        e = jnp.where(adj[None, None] > 0, e, MASK_VAL)
        att = jax.nn.softmax(e, axis=-1)
        h = jnp.einsum('bhij,bhjd->bhid', att, Wh)
        h = h.transpose(0, 2, 1, 3).reshape(B, N, H * hs)
        return jax.nn.elu(h)

    h = jnp.maximum(_layernorm(x, axis=-1), 0.0)
    x = x + _L0_gnn_ref(h, adj, L0_gnn_Wq, L0_gnn_bq, L0_gnn_Wk, L0_gnn_bk, L0_gnn_Wv, L0_gnn_bv, L0_gnn_Wo, L0_gnn_bo, L0_gnn_gamma, L0_gnn_beta)
    h = jnp.maximum(_layernorm(x, axis=-1), 0.0)
    x = x + _L1_gnn_ref(h, adj, L1_gnn_W, L1_gnn_a)
    return x


_drawn_inputs = setup_inputs


def setup_inputs(seed=0):
    import zlib

    import numpy as np

    out = dict(_drawn_inputs(seed))
    spreads = {'L0_gnn_bq': (0.0, 0.8),
     'L0_gnn_bk': (0.0, 0.8),
     'L0_gnn_bv': (0.0, 0.1),
     'L0_gnn_bo': (0.0, 0.418),
     'L0_gnn_gamma': (1.0, 0.2),
     'L0_gnn_beta': (0.0, 0.1)}
    factors = {}
    for name, (base, spread) in spreads.items():
        noise = np.random.default_rng([zlib.crc32(name.encode()), seed]).standard_normal(out[name].shape)
        drawn = base * np.exp(spread * noise) if base else spread * noise
        out[name] = jnp.asarray(drawn.astype(out[name].dtype))
    for name, factor in factors.items():
        out[name] = (out[name] * factor).astype(out[name].dtype)
    return out
```

```python
from contextlib import ExitStack

import concourse.bass as bass
from concourse import mybir

ALU = mybir.AluOpType
ACT = mybir.ActivationFunctionType
AX = mybir.AxisListType
F32 = mybir.dt.float32
F32R = mybir.dt.float32r
BF16 = mybir.dt.bfloat16
I32 = mybir.dt.int32
I8 = mybir.dt.int8

P = 128
F = 256
FH = F // P
N = 2048
NB = 8
H = 4
D = F // H
PAIRS = H // 2
BLK = N // P
TW = 512
T = N // TW
TB = TW // P
CHUNK = 256
KPC = CHUNK // P
CH = N // CHUNK
EPS = 1e-5
CLIP = 10.0
SCALE = D ** -0.5
CLIP_RAW = CLIP / SCALE
MAGIC = 1597463007.0

SPC = PAIRS * KPC
STEPS = CH * SPC
HALF = STEPS // 2
CPH = CH // 2
BSTEPS = T * STEPS
GPH = CPH * PAIRS
LAG = 2
ES = 8
TAIL = HALF
CHAIN_B = T * 13 + T * 13 + 2 * T * 2


def newton(dve, chain, y, a, v):
    chain(dve.tensor_scalar(y.bitcast(I32), v.bitcast(I32), -0.5, MAGIC, ALU.mult, ALU.add))
    for _ in range(3):
        chain(dve.scalar_tensor_tensor(out=a, in0=y, scalar=-0.5, in1=y, op0=ALU.mult, op1=ALU.mult))
        chain(dve.tensor_tensor(a, a, v, ALU.mult))
        chain(dve.scalar_tensor_tensor(out=y, in0=a, scalar=1.5, in1=y, op0=ALU.add, op1=ALU.mult))


def layer0(nc, x, adjT, wqT, wkT, wvT, woT, bq, bk, bv, bo, gamma, beta, x1, nb):
    with ExitStack() as ctx:
        def sb(name, shape, dt=F32):
            return ctx.enter_context(nc.sbuf_tensor(name, shape, dt))

        def ps(name, shape, dt=F32):
            return ctx.enter_context(nc.psum_tensor(name, shape, dt))

        def sem(name):
            return ctx.enter_context(nc.semaphore(name))

        mask = sb("mask", [P, BLK, N], I8)
        w_q, w_k, w_v, w_o = (sb(n, [P, FH, F]) for n in ("w_q", "w_k", "w_v", "w_o"))
        b_q, b_k = sb("b_q", [P, PAIRS]), sb("b_k", [P, PAIRS])
        b_v, b_o, g_row, be_row = (sb(n, [P, F]) for n in ("b_v", "b_o", "g_row", "be_row"))
        ident = sb("ident", [P, P])
        hot = sb("hot", [P, CPH, 32])
        lo_rows = sb("lo_rows", [P, 1])
        pick_f = sb("pick_f", [P, P])
        pick = sb("pick", [P, GPH, P], F32R)
        xin = sb("xin", [P, 2, TB, F])
        hT = sb("hT", [P, FH, N])
        kS = sb("kS", [P, H, N], F32R)
        v_sb = sb("v_sb", [P, BLK, F])
        stats = sb("stats", [P, BLK, 6])
        mv = sb("mv", [P, BLK, 2])
        rs = sb("rs", [P, BLK])
        nmr = sb("nmr", [P, BLK])
        tmp = sb("tmp", [P, BLK])
        qM = sb("qM", [P, 2, 2, H, TW], F32R)
        e_sb = sb("e_sb", [P, ES, 2, TW])
        num = sb("num", [P, GPH, TW])
        r_f = sb("r_f", [P, TW])
        r_hi = sb("r_hi", [P, TW], F32R)
        r_s = sb("r_s", [P, TW], F32R)
        ctxT = sb("ctxT", [P, PAIRS, TW])
        xr = sb("xr", [P, TB, F])
        hy = sb("hy", [P, TB, F])
        st2 = sb("st2", [P, TB, 6])
        mv2 = sb("mv2", [P, TB, 2])
        rs2 = sb("rs2", [P, TB])
        tmp2 = sb("tmp2", [P, TB])
        var2 = sb("var2", [P, TB])

        psS = ps("psS", [P, 2, 2, TW])
        psN = ps("psN", [P, PAIRS, TW])
        psD = ps("psD", [P, TW])
        psM = ps("psM", [P, TW])

        const_in = sem("const_in")
        adj_in = [sem(f"adj_in{i}") for i in range(2)]
        mask_done = sem("mask_done")
        consts_done = sem("consts_done")
        pool_chain = sem("pool_chain")
        x_in = [sem(f"x_in{i}") for i in range(2)]
        dve_chain = sem("dve_chain")
        stats_done = sem("stats_done")
        h_done = sem("h_done")
        tr_done = sem("tr_done")
        hT_done = sem("hT_done")
        kproj_done = sem("kproj_done")
        khi_done = sem("khi_done")
        klo_done = sem("klo_done")
        vproj_done = sem("vproj_done")
        v_done = sem("v_done")
        qproj_done = sem("qproj_done")
        qhi_done = sem("qhi_done")
        qlo_done = sem("qlo_done")
        scores_done = sem("scores_done")
        clip_done = sem("clip_done")
        exp_done = sem("exp_done")
        num_done = sem("num_done")
        numcopy_done = sem("numcopy_done")
        sums_done = sem("sums_done")
        r_read = sem("r_read")
        r_done = sem("r_done")
        bcast_done = sem("bcast_done")
        norm_done = sem("norm_done")
        ctx_done = sem("ctx_done")
        oproj_done = sem("oproj_done")
        xr_in = sem("xr_in")
        hr_done = sem("hr_done")
        hb_done = sem("hb_done")
        y_done = sem("y_done")
        yn_done = sem("yn_done")
        o_done = sem("o_done")
        x1_out = sem("x1_out")

        stage = [e_sb[:, 4 * i:4 * i + 4, :, :].rearrange("p s a w -> p (s a) w").bitcast(I32) for i in range(2)]
        adj_v = adjT.rearrange("(k p) n -> p k n", p=P)
        x_v = x.rearrange("b (t j p) f -> b t p j f", p=P, j=TB)
        x1_v = x1.rearrange("b (t j p) f -> b t p j f", p=P, j=TB)
        NST = BLK // 8 * T
        NCONST = 10

        HALVES = 2 * T

        SUMS = T * (2 * GPH - PAIRS)

        def sums_until(half, i):
            if i < 0:
                return sums_until(half - 1, GPH + i)
            if half % 2 == 0:
                return half * GPH - half // 2 * PAIRS + max(i, i % PAIRS + PAIRS) + 1 - PAIRS
            return half * GPH - (half + 1) // 2 * PAIRS + i + 1

        def halves_before(s):
            return s // HALF - 1, s % HALF

        block = ctx.enter_context(nc.Block())

        @block.sync
        def _(sp):
            for dst, src in ((w_q, wqT), (w_k, wkT), (w_v, wvT), (w_o, woT)):
                sp.dma_start(dst[:, :, :], src.rearrange("(c p) n -> p c n", p=P)).then_inc(const_in, 16)
            sp.dma_start(b_q[:, :], bq).then_inc(const_in, 16)
            sp.dma_start(b_k[:, :], bk).then_inc(const_in, 16)
            for dst, src in ((b_v, bv), (b_o, bo), (g_row, gamma), (be_row, beta)):
                sp.dma_start(dst[:, :], src.partition_broadcast(P)).then_inc(const_in, 16)
            for i in range(NST):
                if i >= 2:
                    sp.wait_ge(mask_done, i - 1)
                t, k = i // 2, i % 2
                sp.dma_start(stage[i % 2], adj_v[:, 8 * k:8 * k + 8, t * TW:(t + 1) * TW])\
                  .then_inc(adj_in[i % 2], 16)
            with sp.Fori(0, nb) as b:
                for t in range(T):
                    if t >= 2:
                        sp.wait_ge(tr_done, b * T + t - 1)
                    sp.dma_start(xin[:, t % 2], x_v[bass.ds(b, 1), t:t + 1].rearrange("o q p j f -> (o q p) j f"))\
                      .then_inc(x_in[t % 2], 16)
                for t in range(T):
                    if t == 0:
                        sp.wait_ge(x1_out, b * (16 * T) + 16)
                    sp.dma_start(xr[:, :, :], x_v[bass.ds(b, 1), t:t + 1].rearrange("o q p j f -> (o q p) j f"))\
                      .then_inc(xr_in, 16)
                    sp.wait_ge(o_done, b * T + t + 1)
                    sp.dma_start(x1_v[bass.ds(b, 1), t:t + 1].rearrange("o q p j f -> (o q p) j f"), hy[:, :, :])\
                      .then_inc(x1_out, 16)
                    if t < T - 1:
                        sp.wait_ge(x1_out, b * (16 * T) + 16 * t + 32)
            sp.wait_ge(x1_out, nb * T * 16 + 16)

        @block.gpsimd
        def _(pool):
            count = [0]

            def chain(ins):
                count[0] += 1
                ins.then_inc(pool_chain, 1)
                pool.wait_ge(pool_chain, count[0])

            pool.memset(tmp[:, :], 0.0).then_inc(x1_out, 16)
            chain(pool.memset(ident[:, :], 0.0))
            chain(pool.affine_select(out=ident[:, :], in_=ident[:, :], compare_op=ALU.not_equal, fill=1.0,
                                     base=0, pattern=[[-1, P]], channel_multiplier=1))
            chain(pool.memset(hot[:, :, :], 0.0))
            for c in range(CPH):
                chain(pool.memset(hot[:, c, :].rearrange("p (a r) -> p a r", r=CPH)[:, :, c], 1.0))
            chain(pool.memset(lo_rows[:, :], 0.0))
            for q in range(H):
                for c in range(CPH):
                    chain(pool.affine_select(out=lo_rows[:, :], in_=lo_rows[:, :], compare_op=ALU.not_equal,
                                             fill=-1.0, base=-(32 * q + CPH + c), pattern=[[0, 1]],
                                             channel_multiplier=1))
            for g in range(GPH):
                c, pair = g // PAIRS, g % PAIRS
                chain(pool.memset(pick_f[:, :], 0.0))
                for i in range(2):
                    for part in range(2):
                        row = 32 * (2 * pair + i) + CPH * part + c
                        chain(pool.affine_select(out=pick_f[:, 64 * i:64 * i + 64],
                                                 in_=pick_f[:, 64 * i:64 * i + 64],
                                                 compare_op=ALU.not_equal, fill=1.0, base=-row,
                                                 pattern=[[0, 64]], channel_multiplier=1))
                chain(pool.tensor_copy(pick[:, g, :], pick_f[:, :]))
            pool.wait_ge(const_in, 16 * NCONST)
            pool.memset(tmp2[:, :], 0.0).then_inc(consts_done, 1)
            with pool.Fori(0, nb) as b:
                for s in range(HALF, BSTEPS + TAIL):
                    half, ss = halves_before(s)
                    t, second = half // 2, half % 2
                    i = ss - 4
                    if 0 <= i < GPH and half < HALVES:
                        pool.wait_ge(norm_done, b * (HALVES * GPH) + half * GPH + i + 1)
                        pair = i % PAIRS
                        if second == 0 and i < 2 * PAIRS:
                            if t >= 1 and i >= PAIRS:
                                pool.wait_ge(oproj_done, b * (2 * T) + 2 * t)
                            if i >= PAIRS:
                                pool.tensor_tensor(ctxT[:, pair, :], num[:, pair, :], num[:, i, :], ALU.add)\
                                    .then_inc(ctx_done, 1)
                        else:
                            pool.wait_ge(ctx_done, b * SUMS + sums_until(half, i - PAIRS))
                            pool.tensor_tensor(ctxT[:, pair, :], ctxT[:, pair, :], num[:, i, :], ALU.add)\
                                .then_inc(ctx_done, 1)
                    if second == 1 and ss == 2:
                        pool.wait_ge(hr_done, b * T + t + 1)
                        pool.tensor_tensor(hy[:, :, :], hy[:, :, :], b_o[:, None, :].to_broadcast([P, TB, F]),
                                           ALU.add).then_inc(hb_done, 1)
                    if second == 1 and ss == HALF - 1:
                        base = 5 * (b * T + t)
                        pool.wait_ge(yn_done, b * T + t + 1)
                        pool.tensor_tensor(hy[:, :, :], hy[:, :, :], g_row[:, None, :].to_broadcast([P, TB, F]),
                                           ALU.mult).then_inc(pool_chain, 1)
                        pool.wait_ge(pool_chain, b * (2 * T) + count[0] + 2 * t + 1)
                        pool.wait_ge(xr_in, b * (16 * T) + 16 * t + 16)
                        pool.tensor_tensor(hy[:, :, :], hy[:, :, :], xr[:, :, :], ALU.add).then_inc(pool_chain, 1)
                        pool.wait_ge(pool_chain, b * (2 * T) + count[0] + 2 * t + 2)
                        pool.tensor_tensor(hy[:, :, :], hy[:, :, :], be_row[:, None, :].to_broadcast([P, TB, F]),
                                           ALU.add).then_inc(o_done, 1)

        @block.scalar
        def _(act):
            for i in range(1, NST, 2):
                act.wait_ge(adj_in[1], 16 * (i // 2 + 1))
                act.wait_ge(mask_done, i)
                t, k = i // 2, i % 2
                act.activation(mask[:, 8 * k:8 * k + 8, t * TW:(t + 1) * TW], stage[1], ACT.Copy,
                               bias=-CLIP_RAW, scale=2 * CLIP_RAW).then_inc(mask_done, 1)
            act.wait_ge(consts_done, 1)

            def q_high(b, t, pair):
                act.wait_ge(qproj_done, b * (T * PAIRS) + t * PAIRS + pair + 1)
                for i in range(2):
                    rows = slice(64 * i, 64 * i + 64)
                    for j in range(2):
                        ins = act.activation(qM[64 * j:64 * j + 64, t % 2, 0, 2 * pair + i, :], psM[rows, :],
                                             ACT.Identity, bias=b_q[rows, pair:pair + 1])
                ins.then_inc(qhi_done, 1)

            with act.Fori(0, nb) as b:
                for t in range(T):
                    act.wait_ge(stats_done, b * T + t + 1)
                    for j in range(TB):
                        n = TB * t + j
                        ins = act.activation(xin[:, t % 2, j, :], xin[:, t % 2, j, :], ACT.Relu,
                                             bias=nmr[:, n:n + 1], scale=rs[:, n:n + 1])
                    ins.then_inc(h_done, 1)
                    act.wait_ge(tr_done, b * T + t + 1)
                    act.activation(hT[:, 1, t * TW:(t + 1) * TW], psS[:, 0, 1, :], ACT.Copy).then_inc(hT_done, 1)
                    for pair in range(PAIRS):
                        act.wait_ge(kproj_done, b * (T * PAIRS) + t * PAIRS + pair + 1)
                        for i in range(2):
                            rows = slice(64 * i, 64 * i + 64)
                            ins = act.activation(kS[rows, 2 * pair + i, t * TW:(t + 1) * TW],
                                                 psS[rows, 1, pair, :], ACT.Identity,
                                                 bias=b_k[rows, pair:pair + 1])
                        ins.then_inc(khi_done, 1)
                for pair in range(PAIRS):
                    q_high(b, 0, pair)
                for s in range(BSTEPS + TAIL):
                    if s < BSTEPS:
                        act.wait_ge(clip_done, b * BSTEPS + s + 1)
                        act.activation(e_sb[:, s % ES], e_sb[:, s % ES], ACT.Exp, scale=SCALE)\
                           .then_inc(exp_done, 1)
                    if s >= 5 and s % 2 == 1 and s < BSTEPS + 4:
                        g = (s - 5) // 2
                        act.wait_ge(num_done, b * (BSTEPS // 2) + g + 1)
                        if g >= GPH:
                            act.wait_ge(ctx_done, b * SUMS + sums_until((g - GPH) // GPH, g % GPH))
                        act.activation(num[:, g % GPH, :], psN[:, g % PAIRS, :], ACT.Copy)\
                           .then_inc(numcopy_done, 1)
                    half, ss = halves_before(s)
                    if half >= 0 and half % 2 == 1 and ss == 0:
                        t = half // 2
                        act.wait_ge(xr_in, b * (16 * T) + 16 * t + 16)
                        for j in range(TB):
                            n = TB * t + j
                            ins = act.activation(hy[:, j, :], xr[:, j, :], ACT.Relu,
                                                 bias=nmr[:, n:n + 1], scale=rs[:, n:n + 1])
                        ins.then_inc(hr_done, 1)
                    if s < BSTEPS and s // HALF % 2 == 1 and s // STEPS < T - 1:
                        if s % HALF in (13, 15):
                            q_high(b, s // STEPS + 1, (s % HALF - 13) // 2)

        @block.vector
        def _(dve):
            count = [0]

            for i in range(0, NST, 2):
                dve.wait_ge(adj_in[0], 16 * (i // 2 + 1))
                if i:
                    dve.wait_ge(mask_done, i)
                t, k = i // 2, i % 2
                dve.tensor_scalar(mask[:, 8 * k:8 * k + 8, t * TW:(t + 1) * TW], stage[0],
                                  2 * CLIP_RAW, -CLIP_RAW, ALU.mult, ALU.add).then_inc(mask_done, 1)
            dve.wait_ge(consts_done, 1)
            dve.wait_ge(mask_done, NST)

            def q_low(b, t, pair, j):
                if j == 0:
                    dve.wait_ge(qhi_done, b * (T * PAIRS) + t * PAIRS + pair + 1)
                for i in range(2):
                    rows = slice(64 * i, 64 * i + 64)
                    hd = 2 * pair + i
                    ins = dve.scalar_tensor_tensor(
                        out=qM[64 * j:64 * j + 64, t % 2, 1, hd, :], in0=psM[rows, :],
                        scalar=b_q[rows, pair:pair + 1], in1=qM[rows, t % 2, 0, hd, :].bitcast(F32),
                        op0=ALU.add, op1=ALU.subtract)
                if j == 1:
                    ins.then_inc(qlo_done, 1)

            with dve.Fori(0, nb) as b:
                count[0] = 0

                def chain(ins, aggr=False):
                    count[0] += 1
                    ins.then_inc(dve_chain, 1)
                    dve.wait_ge(dve_chain, b * CHAIN_B + count[0])
                    if aggr:
                        dve.memset(var2[:, :], 0.0)

                for t in range(T):
                    blocks = slice(TB * t, TB * t + TB)
                    dve.wait_ge(x_in[t % 2], b * (8 * T) + 16 * (t // 2) + 16)
                    for j in range(TB):
                        ins = dve.bn_stats(stats[:, TB * t + j, :], xin[:, t % 2, j, :])
                    chain(ins, True)
                    for j in range(TB):
                        ins = dve.bn_aggr(mv[:, TB * t + j, :], stats[:, TB * t + j, :])
                    chain(ins)
                    chain(dve.tensor_scalar(nmr[:, blocks], mv[:, blocks, 1], EPS, None, ALU.add))
                    newton(dve, chain, rs[:, blocks], tmp[:, blocks], nmr[:, blocks])
                    dve.scalar_tensor_tensor(out=nmr[:, blocks], in0=mv[:, blocks, 0], scalar=-1.0,
                                             in1=rs[:, blocks], op0=ALU.mult, op1=ALU.mult)\
                       .then_inc(stats_done, 1)
                    dve.wait_ge(tr_done, b * T + t + 1)
                    dve.tensor_copy(hT[:, 0, t * TW:(t + 1) * TW], psS[:, 0, 0, :]).then_inc(hT_done, 1)
                    for pair in range(PAIRS):
                        dve.wait_ge(khi_done, b * (T * PAIRS) + t * PAIRS + pair + 1)
                        for i in range(2):
                            rows = slice(64 * i, 64 * i + 64)
                            other = slice(64 - 64 * i, 128 - 64 * i)
                            cols = slice(t * TW, (t + 1) * TW)
                            ins = dve.scalar_tensor_tensor(
                                out=kS[other, 2 * pair + i, cols], in0=psS[rows, 1, pair, :],
                                scalar=b_k[rows, pair:pair + 1],
                                in1=kS[rows, 2 * pair + i, cols].bitcast(F32),
                                op0=ALU.add, op1=ALU.subtract)
                        ins.then_inc(klo_done, 1)
                    for j in range(TB // 2):
                        n = TB * t + 2 * j
                        dve.wait_ge(vproj_done, b * (BLK // 2) + n // 2 + 1)
                        dve.tensor_tensor(v_sb[:, n:n + 2, :],
                                          psN[:, j, :].rearrange("p (a f) -> p a f", a=2),
                                          b_v[:, None, :].to_broadcast([P, 2, F]), ALU.add).then_inc(v_done, 1)
                for pair in range(PAIRS):
                    q_low(b, 0, pair, 0)
                    q_low(b, 0, pair, 1)
                for s in range(BSTEPS + TAIL):
                    if s < BSTEPS:
                        t, kb, pair = s // STEPS, s % STEPS // SPC * KPC + s % KPC, s // KPC % PAIRS
                        if s >= ES:
                            old = s - ES
                            dve.wait_ge(sums_done, b * (BSTEPS // 2) + old // SPC * KPC + old % KPC + 1)
                        dve.wait_ge(scores_done, b * BSTEPS + s + 1)
                        dve.scalar_tensor_tensor(
                            out=e_sb[:, s % ES], in0=psS[:, s % 2], scalar=-CLIP_RAW,
                            in1=mask[:, kb, t * TW:(t + 1) * TW][:, None, :].to_broadcast([P, 2, TW]),
                            op0=ALU.max, op1=ALU.min).then_inc(clip_done, 1)
                    half, ss = halves_before(s)
                    if half >= 0:
                        t, second = half // 2, half % 2
                        if ss == 2:
                            dve.wait_ge(sums_done, b * (BSTEPS // 2) + (half + 1) * CPH * KPC)
                            if half >= 1:
                                dve.wait_ge(bcast_done, b * (HALVES * GPH) + half * GPH)
                            chain(dve.reciprocal(r_f[:, :], psD[:, :]))
                            chain(dve.tensor_copy(r_hi[:, :], r_f[:, :]))
                            dve.scalar_tensor_tensor(out=r_s[:, :], in0=r_hi[:, :].bitcast(F32),
                                                     scalar=lo_rows[:, 0:1], in1=r_f[:, :], op0=ALU.mult,
                                                     op1=ALU.add).then_inc(r_done, 1)
                        i = ss - 4
                        if 0 <= i < GPH:
                            dve.wait_ge(bcast_done, b * (HALVES * GPH) + half * GPH + i + 1)
                            dve.wait_ge(numcopy_done, b * (HALVES * GPH) + half * GPH + i + 1)
                            dve.tensor_tensor(num[:, i, :], num[:, i, :], psM[:, :], ALU.mult)\
                               .then_inc(norm_done, 1)
                        if second == 1 and ss in (13, 15):
                            j = (ss - 13) // 2
                            dve.wait_ge(oproj_done, b * (2 * T) + 2 * t + j + 1)
                            if j == 0:
                                dve.wait_ge(hb_done, b * T + t + 1)
                            ins = dve.tensor_tensor(hy[:, 2 * j:2 * j + 2, :],
                                                    psM[:, :].rearrange("p (a f) -> p a f", a=2),
                                                    hy[:, 2 * j:2 * j + 2, :], ALU.add)
                            ins.then_inc(y_done, 1)
                            if j == 1:
                                dve.wait_ge(y_done, b * (2 * T) + 2 * t + 2)
                                for j in range(TB):
                                    ins = dve.bn_stats(st2[:, j, :], hy[:, j, :])
                                chain(ins, True)
                                for j in range(TB):
                                    ins = dve.bn_aggr(mv2[:, j, :], st2[:, j, :])
                                chain(ins)
                                chain(dve.tensor_scalar(var2[:, :], mv2[:, :, 1], EPS, None, ALU.add))
                                newton(dve, chain, rs2[:, :], tmp2[:, :], var2[:, :])
                                for j in range(TB):
                                    ins = dve.tensor_scalar(hy[:, j, :], hy[:, j, :], mv2[:, j, 0:1],
                                                            rs2[:, j:j + 1], ALU.subtract, ALU.mult)
                                ins.then_inc(yn_done, 1)
                    if s < BSTEPS and s // HALF % 2 == 1 and s // STEPS < T - 1:
                        if s % HALF in (13, 15):
                            q_low(b, s // STEPS + 1, (s % HALF - 13) // 2, 0)
                            q_low(b, s // STEPS + 1, (s % HALF - 13) // 2, 1)
                assert count[0] == CHAIN_B, count[0]

        @block.tensor
        def _(pe):
            pe.wait_ge(consts_done, 1)

            def q_proj(b, t, pair):
                for c in range(FH):
                    ins = pe.matmul(psM[:, :], w_q[:, c, pair * P:(pair + 1) * P],
                                    hT[:, c, t * TW:(t + 1) * TW], start=c == 0, stop=c == FH - 1)
                ins.then_inc(qproj_done, 1)

            with pe.Fori(0, nb) as b:
                for t in range(T):
                    cols = slice(t * TW, (t + 1) * TW)
                    pe.wait_ge(h_done, b * T + t + 1)
                    if t:
                        pe.wait_ge(hT_done, b * (2 * T) + 2 * t)
                    for c in range(FH):
                        for j in range(TB):
                            ins = pe.transpose(psS[:, 0, c, j * P:(j + 1) * P],
                                               xin[:, t % 2, j, c * P:(c + 1) * P], ident[:, :])
                    ins.then_inc(tr_done, 1)
                    pe.wait_ge(hT_done, b * (2 * T) + 2 * t + 2)
                    for pair in range(PAIRS):
                        if t:
                            pe.wait_ge(klo_done, b * (T * PAIRS) + (t - 1) * PAIRS + pair + 1)
                        for c in range(FH):
                            ins = pe.matmul(psS[:, 1, pair, :], w_k[:, c, pair * P:(pair + 1) * P],
                                            hT[:, c, cols], start=c == 0, stop=c == FH - 1)
                        ins.then_inc(kproj_done, 1)
                    for j in range(TB // 2):
                        n = TB * t + 2 * j
                        if t:
                            pe.wait_ge(v_done, b * (BLK // 2) + n // 2 - 1)
                        for a in range(2):
                            for c in range(FH):
                                ins = pe.matmul(psN[:, j, a * F:(a + 1) * F],
                                                hT[:, c, (n + a) * P:(n + a + 1) * P], w_v[:, c, :],
                                                start=c == 0, stop=c == FH - 1)
                        ins.then_inc(vproj_done, 1)
                for pair in range(PAIRS):
                    if pair:
                        pe.wait_ge(qlo_done, b * (T * PAIRS) + pair)
                    q_proj(b, 0, pair)
                pe.wait_ge(klo_done, (b + 1) * (T * PAIRS))
                pe.wait_ge(v_done, (b + 1) * (BLK // 2))
                for s in range(BSTEPS + TAIL):
                    if s < BSTEPS:
                        t, kb, pair = s // STEPS, s % STEPS // SPC * KPC + s % KPC, s // KPC % PAIRS
                        if s >= 2:
                            pe.wait_ge(clip_done, b * BSTEPS + s - 1)
                        if s % STEPS in (0, KPC):
                            pe.wait_ge(qlo_done, b * (T * PAIRS) + t * PAIRS + pair + 1)
                        for i in range(2):
                            hd = 2 * pair + i
                            for part in range(2):
                                ins = pe.matmul(psS[:, s % 2, i, :], kS[:, hd, kb * P:(kb + 1) * P],
                                                qM[:, t % 2, part, hd, :], start=part == 0, stop=part == 1)
                        ins.then_inc(scores_done, 1)
                    u = s - LAG
                    if 0 <= u < BSTEPS:
                        kb, pair, g = u % STEPS // SPC * KPC + u % KPC, u // KPC % PAIRS, u // KPC
                        pe.wait_ge(exp_done, b * BSTEPS + u + 1)
                        if u % KPC == 0 and g >= PAIRS:
                            pe.wait_ge(numcopy_done, b * (BSTEPS // 2) + g - 1)
                        for i in range(2):
                            hd = 2 * pair + i
                            ins = pe.matmul(psN[64 * i:64 * i + 64, pair, :], v_sb[:, kb, hd * D:(hd + 1) * D],
                                            e_sb[:, u % ES, i, :], start=u % KPC == 0, stop=u % KPC == KPC - 1,
                                            skip_group_check=True)
                        if u % KPC == KPC - 1:
                            ins.then_inc(num_done, 1)
                        if pair == PAIRS - 1:
                            c = u // SPC % CPH
                            first, last = u % HALF == KPC, u % HALF == HALF - 1
                            if first and u >= HALF:
                                pe.wait_ge(r_done, b * HALVES + u // HALF)
                            for hd in range(H):
                                slot = (u - KPC * (PAIRS - 1 - hd // 2)) % ES
                                ins = pe.matmul(psD[32 * hd:32 * hd + 32, :], hot[:, c, :],
                                                e_sb[:, slot, hd % 2, :], start=first, stop=last,
                                                skip_group_check=True)
                            ins.then_inc(sums_done, 1)
                    half, ss = halves_before(s)
                    if half >= 0:
                        t, second = half // 2, half % 2
                        i = ss - 3
                        if 0 <= i < GPH:
                            if i == 0:
                                pe.wait_ge(r_done, b * HALVES + half + 1)
                            else:
                                pe.wait_ge(norm_done, b * (HALVES * GPH) + half * GPH + i)
                            pe.matmul(psM[:, :], pick[:, i, :], r_s[:, :], start=True, stop=True)\
                              .then_inc(bcast_done, 1)
                        if second == 1 and ss in (12, 14):
                            j = (ss - 12) // 2
                            if j == 0:
                                pe.wait_ge(ctx_done, b * SUMS + sums_until(half, GPH - 1))
                            else:
                                pe.wait_ge(y_done, b * (2 * T) + 2 * t + 1)
                            for a in range(2):
                                col = (2 * j + a) * P
                                for pair in range(PAIRS):
                                    ins = pe.matmul(psM[:, a * F:(a + 1) * F], ctxT[:, pair, col:col + P],
                                                    w_o[:, pair, :], start=pair == 0, stop=pair == PAIRS - 1)
                            ins.then_inc(oproj_done, 1)
                    if s < BSTEPS and s // HALF % 2 == 1 and s // STEPS < T - 1:
                        if s % HALF in (12, 14):
                            t, pair = s // STEPS + 1, (s % HALF - 12) // 2
                            if pair == 0:
                                pe.wait_ge(norm_done, b * (HALVES * GPH) + (s // HALF) * GPH)
                            else:
                                pe.wait_ge(qlo_done, b * (T * PAIRS) + t * PAIRS + pair)
                            q_proj(b, t, pair)


W1 = D + 2
XW = D + 1
PARTS = 3
KC = 4
KCH = BLK // KC
ALPHA = 0.2
BIG = 2.0 ** 60
SHIFT = 60.0
CHAIN1_P = T * 13
CHAIN1_X = 4


def layer1(nc, x1, adjT, w, a1, a2, out, nb):
    with ExitStack() as ctx:
        def sb(name, shape, dt=F32):
            return ctx.enter_context(nc.sbuf_tensor(name, shape, dt))

        def ps(name, shape, dt=F32):
            return ctx.enter_context(nc.psum_tensor(name, shape, dt))

        def sem(name):
            return ctx.enter_context(nc.semaphore(name))

        adj = sb("adj", [P, BLK, N], BF16)
        w_all = sb("w_all", [P, FH, H, W1])
        w_ei = sb("w_ei", [P, FH, H, P])
        ident = sb("ident1", [P, P])
        ones = sb("ones1", [H, P])
        xin = sb("xin1", [P, 2, TB, F])
        stats = sb("stats1", [P, TB, 6])
        mv = sb("mv1", [P, TB, 2])
        rs = sb("rs1", [P, 2, TB])
        nmr = sb("nmr1", [P, 2, TB])
        var = sb("var1", [P, TB])
        tmp = sb("tmp1", [P, TB])
        hT = sb("hT1", [P, FH, N])
        wh = sb("wh", [P, BLK, H, W1])
        mx_p = sb("mx_p", [P, H])
        mx = sb("mx", [H, 1])
        mx_d = sb("mx_d", [H, H])
        cen = sb("cen", [P, H])
        xq = sb("xq", [P, 2, BLK, H])
        cq = sb("cq", [P, 2, BLK, H])
        bigj = sb("bigj", [P, BLK, H])
        xf = sb("xf", [P, 2, BLK, XW])
        xy = sb("xy", [P, H, 2, BLK, PARTS, XW], BF16)
        pos = sb("pos", [P, KCH, KC, TW], BF16)
        neg = sb("neg", [P, KCH, KC, TW], BF16)
        red = sb("red", [P, 2, TB, 2, XW])
        rden = sb("rden", [P, 2, TB])
        o_sb = sb("o_sb", [P, BLK, F])

        psP = ps("psP", [P, 2, TW])
        psE = ps("psE", [P, 2, TW])
        psA = ps("psA", [P, TB, TW])

        const_in = sem("const1_in")
        adj_in = [sem(f"adj1_in{i}") for i in range(2)]
        adj_done = sem("adj1_done")
        ident_done = sem("ident1_done")
        w_done = sem("w1_done")
        w_chain = sem("w1_chain")
        x_in = [sem(f"x1_in{i}") for i in range(2)]
        dve_chain = sem("dve1_chain")
        stats_done = sem("stats1_done")
        h_done = sem("h1_done")
        tr_done = sem("tr1_done")
        hT_done = sem("hT1_done")
        wh_proj = sem("wh_proj")
        wh_done = sem("wh_done")
        mx_part = sem("mx_part")
        mx_turned = sem("mx_turned")
        mx_diag = sem("mx_diag")
        mx_done = sem("mx_done")
        d_done = sem("d_done")
        q_done = sem("q_done")
        xf_done = sem("xf_done")
        hi_done = sem("hi1_done")
        rest_done = sem("rest_done")
        mid_done = sem("mid_done")
        xy_done = sem("xy_done")
        ei_done = sem("ei_done")
        step_done = sem("step_done")
        pos_done = sem("pos_done")
        neg_done = sem("neg_done")
        piece_free = sem("piece_free")
        acc_done = sem("acc_done")
        red_done = sem("red_done")
        mix_chain = sem("mix_chain")
        mix_done = sem("mix_done")
        rden_done = sem("rden_done")
        o_done = sem("o1_done")
        xo_in = sem("xo_in")
        minus_done = sem("minus_done")
        en_done = sem("en_done")
        fin_chain = sem("fin_chain")
        fin_done = sem("fin_done")
        out_done = sem("out_done")

        adj_v = adjT.rearrange("(k p) n -> p k n", p=P)
        x_v = x1.rearrange("b (t j p) f -> b t p j f", p=P, j=TB)
        out_v = out.rearrange("b (t j p) f -> b t p j f", p=P, j=TB)
        NST = 2 * T
        stage = [t.rearrange("p a k w -> p (a k w)").bitcast(I32).rearrange("p (k w) -> p k w", w=TW)
                 for t in (pos[:, :, :, :], neg[:, :, :, :])]
        U = H * T

        def tile_of(v, b, t):
            return v[bass.ds(b, 1), t:t + 1].rearrange("o q p j f -> (o q p) j f")

        block = ctx.enter_context(nc.Block())

        @block.sync
        def _(sp):
            for c in range(FH):
                sp.dma_start(w_all[:, c, :, 0:D], w[c * P:(c + 1) * P, :, :]).then_inc(const_in, 16)
            sp.dma_start(xf[:, 0, 0:H, 0:D], a1.partition_broadcast(P)).then_inc(const_in, 16)
            sp.dma_start(xf[:, 0, H:2 * H, 0:D], a2.partition_broadcast(P)).then_inc(const_in, 16)
            for i in range(NST):
                if i >= 2:
                    sp.wait_ge(adj_done, i - 1)
                t, k = i // 2, i % 2
                sp.dma_start(stage[i % 2], adj_v[:, 8 * k:8 * k + 8, t * TW:(t + 1) * TW])\
                  .then_inc(adj_in[i % 2], 16)
            with sp.Fori(0, nb) as b:
                for t in range(T):
                    if t == 0:
                        sp.wait_ge(out_done, b * (16 * T) + 16)
                    if t >= 2:
                        sp.wait_ge(tr_done, b * T + t - 1)
                    sp.dma_start(xin[:, t % 2], tile_of(x_v, b, t)).then_inc(x_in[t % 2], 16)
                sp.wait_ge(tr_done, b * T + T)
                for t in range(T):
                    if t >= 1:
                        sp.wait_ge(fin_done, b * T + t)
                        sp.dma_start(tile_of(out_v, b, t - 1), o_sb[:, TB * (t - 1):TB * t, :])\
                          .then_inc(out_done, 16)
                    sp.dma_start(xin[:, 0], tile_of(x_v, b, t)).then_inc(xo_in, 16)
                sp.wait_ge(fin_done, b * T + T)
                sp.dma_start(tile_of(out_v, b, T - 1), o_sb[:, TB * (T - 1):TB * T, :]).then_inc(out_done, 16)
            sp.wait_ge(out_done, nb * T * 16 + 16)

        @block.gpsimd
        def _(pool):
            pool.memset(ones[:, :], 1.0).then_inc(out_done, 16)
            pool.memset(ident[:, :], 0.0).then_inc(ident_done, 1)
            pool.wait_ge(ident_done, 1)
            pool.affine_select(out=ident[:, :], in_=ident[:, :], compare_op=ALU.not_equal, fill=1.0,
                               base=0, pattern=[[-1, P]], channel_multiplier=1).then_inc(ident_done, 1)
            with pool.Fori(0, nb) as b:
                with pool.Fori(0, T) as t:
                    for hd in range(H):
                        unit = b * U + t * H + hd
                        pool.wait_ge(red_done, (unit + 1) * TB + TB)
                        r = red[:, hd % 2]
                        for br in range(2):
                            ins = pool.tensor_tensor(
                                r[:, :, br, :], r[:, :, br, :],
                                cq[:, br, bass.ds(t * TB, TB), hd][:, :, None].to_broadcast([P, TB, XW]), ALU.mult)
                        ins.then_inc(mix_chain, 1)
                        pool.wait_ge(mix_chain, unit + 1)
                        pool.tensor_tensor(r[:, :, 0, :], r[:, :, 0, :], r[:, :, 1, :], ALU.add)\
                            .then_inc(mix_done, 1)
                        pool.wait_ge(rden_done, unit + 1)
                        pool.tensor_tensor(
                            o_sb[:, bass.ds(t * TB, TB), hd * D:(hd + 1) * D], r[:, :, 0, 0:D],
                            rden[:, hd % 2, :][:, :, None].to_broadcast([P, TB, D]), ALU.mult).then_inc(o_done, 1)
                for t in range(T):
                    rows = slice(TB * t, TB * t + TB)
                    pool.wait_ge(en_done, b * T + t + 1)
                    pool.wait_ge(xo_in, b * (16 * T) + 16 * t + 16)
                    pool.tensor_tensor(xin[:, 1], xin[:, 1], xin[:, 0], ALU.add).then_inc(fin_chain, 1)
                    pool.tensor_scalar(o_sb[:, rows, :], o_sb[:, rows, :], 0.0, -1.0, ALU.max, ALU.add)\
                        .then_inc(fin_chain, 1)
                    pool.wait_ge(fin_chain, b * (2 * T) + 2 * t + 2)
                    pool.tensor_tensor(o_sb[:, rows, :], o_sb[:, rows, :], xin[:, 1], ALU.add).then_inc(fin_done, 1)

        @block.scalar
        def _(act):
            for i in range(1, NST, 2):
                act.wait_ge(adj_in[1], 16 * (i // 2 + 1))
                act.wait_ge(adj_done, i)
                t, k = i // 2, i % 2
                act.activation(adj[:, 8 * k:8 * k + 8, t * TW:(t + 1) * TW], stage[1], ACT.Copy).then_inc(adj_done, 1)
            with act.Fori(0, nb) as b:
                for t in range(T):
                    act.wait_ge(stats_done, b * T + t + 1)
                    for j in range(TB):
                        ins = act.activation(xin[:, t % 2, j, :], xin[:, t % 2, j, :], ACT.Relu,
                                             bias=nmr[:, t % 2, j:j + 1], scale=rs[:, t % 2, j:j + 1])
                    ins.then_inc(h_done, 1)
                    act.wait_ge(tr_done, b * T + t + 1)
                    act.activation(hT[:, 1, t * TW:(t + 1) * TW], psP[:, 1, :], ACT.Copy).then_inc(hT_done, 1)
                    for j in range(0, TB, 2):
                        n = TB * t + j
                        act.wait_ge(wh_proj, b * BLK + n + 1)
                        if n:
                            act.wait_ge(wh_done, b * BLK + n)
                        act.activation(wh[:, n].rearrange("p h e -> p (h e)"), psE[:, 0, 0:H * W1], ACT.Copy)\
                           .then_inc(wh_done, 1)
                act.wait_ge(d_done, b + 1)
                act.activation(xq[:, 1], xq[:, 0], ACT.Exp, scale=ALPHA)
                act.activation(xq[:, 0], xq[:, 0], ACT.Exp)
                act.activation(cq[:, 0], cq[:, 0], ACT.Exp, scale=1.0 - ALPHA)
                act.activation(cq[:, 1], cq[:, 1], ACT.Exp, scale=ALPHA - 1.0).then_inc(q_done, 1)
                for hd in range(H):
                    for br in range(2):
                        n = b * (2 * H) + 2 * hd + br
                        act.wait_ge(xf_done, n + 1)
                        act.activation(xy[:, hd, br, :, 0, :], xf[:, br], ACT.Copy).then_inc(hi_done, 1)
                        act.wait_ge(rest_done, n + 1)
                        act.activation(xy[:, hd, br, :, 1, :], xf[:, br], ACT.Copy).then_inc(mid_done, 1)
                with act.Fori(0, T) as t:
                    for hd in range(H):
                        unit = b * U + t * H + hd
                        act.wait_ge(ei_done, unit + 1)
                        for kb in range(BLK):
                            c = kb // KC
                            if kb % KC == 0:
                                if c < KCH - 1:
                                    act.wait_ge(piece_free, unit * (KCH - 1) + c + 1)
                                else:
                                    act.wait_ge(acc_done, unit * TB)
                            ins = act.activation(pos[:, c, kb % KC, :], psE[:, hd % 2, :], ACT.Sigmoid,
                                                 bias=bigj[:, kb, hd:hd + 1], scale=BIG)
                            if kb % KC == KC - 1:
                                ins.then_inc(step_done, 1)
                for t in range(T):
                    act.wait_ge(o_done, b * U + U + 1)
                    if t:
                        act.wait_ge(fin_done, b * T + t)
                    act.activation(xin[:, 1], o_sb[:, TB * t:TB * t + TB, :], ACT.Relu, scale=-1.0)\
                       .then_inc(minus_done, 1)
                    act.wait_ge(minus_done, b * T + t + 1)
                    act.activation(xin[:, 1], xin[:, 1], ACT.Exp, scale=-1.0).then_inc(en_done, 1)

        @block.vector
        def _(dve):
            for i in range(0, NST, 2):
                dve.wait_ge(adj_in[0], 16 * (i // 2 + 1))
                if i:
                    dve.wait_ge(adj_done, i)
                t, k = i // 2, i % 2
                dve.tensor_copy(adj[:, 8 * k:8 * k + 8, t * TW:(t + 1) * TW], stage[0]).then_inc(adj_done, 1)
            dve.wait_ge(const_in, 64)
            n = 0
            for c in range(FH):
                for part in range(2):
                    dve.tensor_tensor(xf[:, 1, 0:H, 0:D], w_all[:, c, :, 0:D], xf[:, 0, part * H:part * H + H, 0:D],
                                      ALU.mult).then_inc(w_chain, 1)
                    dve.wait_ge(w_chain, n + 1)
                    dve.tensor_reduce(w_all[:, c, :, D + part], xf[:, 1, 0:H, 0:D], AX.X, ALU.add)\
                       .then_inc(w_chain, 1)
                    dve.wait_ge(w_chain, n + 2)
                    n += 2
                for hd in range(H):
                    ins = dve.tensor_copy(w_ei[:, c, hd, :], w_all[:, c, hd, D:D + 1].to_broadcast([P, P]))
            ins.then_inc(w_done, 1)
            dve.wait_ge(adj_done, NST)
            dve.memset(rden[:, 0, :], 1.0).then_inc(piece_free, KCH - 1)
            dve.memset(rden[:, 1, :], 1.0).then_inc(red_done, TB)
            dve.memset(mv[:, :, :], 0.0).then_inc(o_done, 1)
            CHAIN = CHAIN1_P + CHAIN1_X

            with dve.Fori(0, nb) as b:
                count = [0]

                def chain(ins, aggr=False):
                    count[0] += 1
                    ins.then_inc(dve_chain, 1)
                    dve.wait_ge(dve_chain, b * CHAIN + count[0])
                    if aggr:
                        dve.memset(var[:, :], 0.0)

                for t in range(T):
                    dve.wait_ge(x_in[t % 2], b * (8 * T) + 16 * (t // 2) + 16)
                    for j in range(TB):
                        ins = dve.bn_stats(stats[:, j, :], xin[:, t % 2, j, :])
                    chain(ins, True)
                    for j in range(TB):
                        ins = dve.bn_aggr(mv[:, j, :], stats[:, j, :])
                    chain(ins)
                    chain(dve.tensor_scalar(var[:, :], mv[:, :, 1], EPS, None, ALU.add))
                    newton(dve, chain, rs[:, t % 2], tmp[:, :], var[:, :])
                    dve.scalar_tensor_tensor(out=nmr[:, t % 2], in0=mv[:, :, 0], scalar=-1.0, in1=rs[:, t % 2],
                                             op0=ALU.mult, op1=ALU.mult).then_inc(stats_done, 1)
                    dve.wait_ge(tr_done, b * T + t + 1)
                    dve.tensor_copy(hT[:, 0, t * TW:(t + 1) * TW], psP[:, 0, :]).then_inc(hT_done, 1)
                    for j in range(1, TB, 2):
                        n = TB * t + j
                        dve.wait_ge(wh_proj, b * BLK + n + 1)
                        dve.wait_ge(wh_done, b * BLK + n)
                        dve.tensor_copy(wh[:, n].rearrange("p h e -> p (h e)"), psE[:, 1, 0:H * W1])\
                           .then_inc(wh_done, 1)
                dve.wait_ge(wh_done, b * BLK + BLK)
                ei, ej = wh[:, :, :, D], wh[:, :, :, D + 1]
                dve.tensor_reduce(mx_p[:, :], ej.rearrange("p k h -> p h k"), AX.X, ALU.max).then_inc(mx_part, 1)
                dve.tensor_scalar(bigj[:, :, :], ej, BIG, None, ALU.mult)
                dve.wait_ge(mx_turned, b + 1)
                chain(dve.tensor_reduce(mx[:, :], psP[0:H, 0, 0:P], AX.X, ALU.max))
                dve.tensor_scalar(mx_d[:, :], ident[0:H, 0:H], mx[:, 0:1], None, ALU.mult).then_inc(mx_diag, 1)
                dve.wait_ge(mx_done, b + 1)
                chain(dve.tensor_scalar(cen[:, :], psP[:, 1, 0:H], -SHIFT, None, ALU.add))
                cen_bc = cen[:, None, :].to_broadcast([P, BLK, H])
                dve.tensor_tensor(xq[:, 0], ej, cen_bc, ALU.subtract)
                chain(dve.tensor_tensor(cq[:, 1], ei, cen_bc, ALU.add))
                chain(dve.tensor_scalar(cq[:, 0], cq[:, 1], 0.0, None, ALU.min))
                dve.tensor_scalar(cq[:, 1], cq[:, 1], 0.0, None, ALU.max).then_inc(d_done, 1)
                dve.wait_ge(q_done, b + 1)
                for hd in range(H):
                    for br in range(2):
                        n = b * (2 * H) + 2 * hd + br
                        f, hi, mid, lo = xf[:, br], *(xy[:, hd, br, :, i, :] for i in range(PARTS))
                        if hd:
                            dve.wait_ge(xy_done, n - 1)
                        dve.tensor_tensor(f[:, :, 0:D], wh[:, :, hd, 0:D],
                                          xq[:, br, :, hd][:, :, None].to_broadcast([P, BLK, D]), ALU.mult)
                        dve.tensor_copy(f[:, :, D:XW], xq[:, br, :, hd][:, :, None]).then_inc(xf_done, 1)
                        dve.wait_ge(hi_done, n + 1)
                        dve.tensor_tensor(f, f, hi, ALU.subtract).then_inc(rest_done, 1)
                        dve.wait_ge(mid_done, n + 1)
                        dve.tensor_tensor(lo, f, mid, ALU.subtract).then_inc(xy_done, 1)
                def piece(unit, t, c):
                    dve.wait_ge(step_done, unit * KCH + c + 1)
                    edges = adj[:, KC * c:KC * c + KC, bass.ds(t * TW, TW)]
                    dve.tensor_tensor(pos[:, c], pos[:, c], edges, ALU.mult).then_inc(pos_done, 1)
                    dve.wait_ge(pos_done, unit * KCH + c + 1)
                    dve.tensor_tensor(neg[:, c], edges, pos[:, c], ALU.subtract).then_inc(neg_done, 1)

                def reduce(unit, hd):
                    dve.wait_ge(o_done, unit + 1)
                    for j in range(TB):
                        dve.wait_ge(acc_done, unit * TB + j + 1)
                        dve.tensor_reduce(
                            red[:, hd % 2, j], psA[:, j, 0:2 * PARTS * XW].rearrange(
                                "p (r c e) -> p r e c", r=2, c=PARTS), AX.X, ALU.add).then_inc(red_done, 1)

                def invert(unit, hd):
                    dve.wait_ge(mix_done, unit + 1)
                    dve.reciprocal(rden[:, hd % 2, :], red[:, hd % 2, :, 0, D]).then_inc(rden_done, 1)

                def tile(t, first):
                    for hd in range(H):
                        unit = b * U + t * H + hd
                        for c in range(KCH):
                            if c == KCH - 1 and not (first and hd == 0):
                                reduce(unit - 1, hd - 1)
                            piece(unit, t, c)
                        if not (first and hd == 0):
                            invert(unit - 1, hd - 1)

                tile(0, True)
                with dve.Fori(1, T) as t:
                    tile(t, False)
                reduce(b * U + U - 1, H - 1)
                invert(b * U + U - 1, H - 1)

        @block.tensor
        def _(pe):
            pe.wait_ge(w_done, 1)
            pe.wait_ge(ident_done, 2)
            with pe.Fori(0, nb) as b:
                for t in range(T):
                    pe.wait_ge(h_done, b * T + t + 1)
                    if t:
                        pe.wait_ge(hT_done, b * (2 * T) + 2 * t)
                    for c in range(FH):
                        for j in range(TB):
                            ins = pe.transpose(psP[:, c, j * P:(j + 1) * P], xin[:, t % 2, j, c * P:(c + 1) * P],
                                               ident[:, :])
                    ins.then_inc(tr_done, 1)
                    pe.wait_ge(hT_done, b * (2 * T) + 2 * t + 2)
                    for j in range(TB):
                        n = TB * t + j
                        if n >= 2:
                            pe.wait_ge(wh_done, b * BLK + n - 1)
                        for c in range(FH):
                            ins = pe.matmul(psE[:, j % 2, 0:H * W1], hT[:, c, n * P:(n + 1) * P],
                                            w_all[:, c].rearrange("p h e -> p (h e)"), start=c == 0, stop=c == FH - 1)
                        ins.then_inc(wh_proj, 1)
                pe.wait_ge(mx_part, b + 1)
                pe.transpose(psP[0:H, 0, 0:P], mx_p[:, :], ident[:, :]).then_inc(mx_turned, 1)
                pe.wait_ge(mx_diag, b + 1)
                pe.matmul(psP[:, 1, 0:H], ones[:, :], mx_d[:, :], start=True, stop=True).then_inc(mx_done, 1)
                pe.wait_ge(xy_done, b * (2 * H) + 2 * H)

                def scores_of_queries(t, hd):
                    for c in range(FH):
                        ins = pe.matmul(psE[:, hd % 2, :], w_ei[:, c, hd, :], hT[:, c, bass.ds(t * TW, TW)],
                                        start=c == 0, stop=c == FH - 1)
                    ins.then_inc(ei_done, 1)

                def tile(t, last):
                    for hd in range(H):
                        unit = b * U + t * H + hd
                        for c in range(KCH):
                            pe.wait_ge(neg_done, unit * KCH + c + 1)
                            if c == 1 and not (last and hd == H - 1):
                                scores_of_queries(t + (hd + 1) // H, (hd + 1) % H)
                            for j in range(TB):
                                if c == 0:
                                    pe.wait_ge(red_done, unit * TB + j + 1)
                                for k in range(KC):
                                    kb = KC * c + k
                                    for br, part in enumerate((pos, neg)):
                                        ins = pe.matmul(
                                            psA[:, j, br * PARTS * XW:(br + 1) * PARTS * XW],
                                            part[:, c, k, j * P:(j + 1) * P],
                                            xy[:, hd, br, kb].rearrange("p c e -> p (c e)"),
                                            start=kb == 0 and br == 0, stop=kb == BLK - 1,
                                            skip_group_check=True)
                                if c == KCH - 1:
                                    ins.then_inc(acc_done, 1)
                            if c < KCH - 1:
                                ins.then_inc(piece_free, 1)

                scores_of_queries(0, 0)
                with pe.Fori(0, T - 1) as t:
                    tile(t, False)
                tile(T - 1, True)


def build(nc, x, adjT, wqT, wkT, wvT, woT, bq, bk, bv, bo, gamma, beta, w, a1, a2, out):
    x1 = nc.dram_tensor("x_between", [NB, N, F], F32).ap()
    layer0(nc, x, adjT, wqT, wkT, wvT, woT, bq, bk, bv, bo, gamma, beta, x1, NB)
    layer1(nc, x1, adjT, w, a1, a2, out, NB)


def kernel(**inputs):
    import numpy as np
    import concourse.bacc as bacc
    from concourse.bass_utils import run_bass_kernel_spmd

    given = {k: np.asarray(v) for k, v in inputs.items()}
    L0 = {k[7:]: v for k, v in given.items() if k.startswith("L0_gnn_")}
    W, a = given["L1_gnn_W"], given["L1_gnn_a"]
    laid_out = {
        "x": given["x"], "adjT": given["adj"].T,
        "wqT": L0["Wq"].T, "wkT": L0["Wk"].T, "wvT": L0["Wv"].T, "woT": L0["Wo"].T,
        "bq": L0["bq"].reshape(PAIRS, P).T, "bk": L0["bk"].reshape(PAIRS, P).T,
        "bv": L0["bv"], "bo": L0["bo"], "gamma": L0["gamma"], "beta": L0["beta"],
        "w": W.transpose(1, 0, 2), "a1": a[:, :D], "a2": a[:, D:],
    }
    nc = bacc.Bacc("TRN2", target_bir_lowering=False, num_devices=1, dynamic_dma_scratch_size=1024)
    arrays, args = {}, []
    for name, v in laid_out.items():
        arrays[name] = np.ascontiguousarray(v)
        args.append(nc.dram_tensor(name, v.shape, mybir.dt.from_np(v.dtype), kind="ExternalInput").ap())
    args.append(nc.dram_tensor("out", (NB, N, F), F32, kind="ExternalOutput").ap())
    build(nc, *args)
    r = run_bass_kernel_spmd(nc, [arrays], core_ids=[0])
    return r.results[0]["out"]
```

```python
from contextlib import ExitStack

import concourse.bass as bass
from concourse import mybir

ALU = mybir.AluOpType
ACT = mybir.ActivationFunctionType
AX = mybir.AxisListType
F32 = mybir.dt.float32
F32R = mybir.dt.float32r
BF16 = mybir.dt.bfloat16
I32 = mybir.dt.int32
I8 = mybir.dt.int8

P = 128
F = 256
FH = F // P
N = 2048
NB = 8
H = 4
D = F // H
PAIRS = H // 2
BLK = N // P
TW = 512
T = N // TW
TB = TW // P
CHUNK = 256
KPC = CHUNK // P
CH = N // CHUNK
EPS = 1e-5
CLIP = 10.0
SCALE = D ** -0.5
CLIP_RAW = CLIP / SCALE
MAGIC = 1597463007.0

SPC = PAIRS * KPC
STEPS = CH * SPC
HALF = STEPS // 2
CPH = CH // 2
BSTEPS = T * STEPS
GPH = CPH * PAIRS
NCONST = 10
LAG = 2
ES = 6
NS = GPH + 4
LN = 13
SUMS_AT, INV_AT, SPLIT_AT, PICK_AT = 2, 2, 6, 7
PROJ_AT, LN_AT = 2, 6
TAIL = HALF + LN_AT + 4
STATS_AT = (-16, -10, 8, 13)
H_AT = (-14, -8, 9, 14)
TR_AT = (2, 7, 12, 17)
Q_AT = 22


def ln_moments(dve, link, mv, stats, eps_var, rows, n):
    for j in range(n):
        ins = dve.bn_stats(stats[:, j, :], rows(j))
    link(ins)
    dve.memset(eps_var, 0.0)
    for j in range(n):
        ins = dve.bn_aggr(mv[:, j, :], stats[:, j, :])
    link(ins)


def ln_rsqrt(dve, link, y, a, eps_var, mv):
    link(dve.tensor_scalar(eps_var, mv[:, :, 1], EPS, None, ALU.add))
    link(dve.tensor_scalar(y.bitcast(I32), eps_var.bitcast(I32), -0.5, MAGIC, ALU.mult, ALU.add))
    for _ in range(3):
        link(dve.scalar_tensor_tensor(out=a, in0=y, scalar=-0.5, in1=y, op0=ALU.mult, op1=ALU.mult))
        link(dve.tensor_tensor(a, a, eps_var, ALU.mult))
        link(dve.scalar_tensor_tensor(out=y, in0=a, scalar=1.5, in1=y, op0=ALU.add, op1=ALU.mult))


def layer0(nc, mask, x, adjT, wqT, wkT, wvT, woT, bq, bk, bv, bo, gamma, beta, x1, nb):
    with ExitStack() as ctx:
        def sb(name, shape, dt=F32):
            return ctx.enter_context(nc.sbuf_tensor(name, shape, dt))

        def ps(name, shape, dt=F32):
            return ctx.enter_context(nc.psum_tensor(name, shape, dt))

        def sem(name):
            return ctx.enter_context(nc.semaphore(name))

        w_q, w_k, w_v, w_o = (sb(n, [P, FH, F]) for n in ("w_q", "w_k", "w_v", "w_o"))
        b_q, b_k = sb("b_q", [P, PAIRS]), sb("b_k", [P, PAIRS])
        b_v, b_o, g_row, be_row = (sb(n, [P, F]) for n in ("b_v", "b_o", "g_row", "be_row"))
        ident = sb("ident", [P, P])
        hot = sb("hot", [P, CPH, 32])
        lo_rows = sb("lo_rows", [P, 1])
        pick_f = sb("pick_f", [P, P])
        pick = sb("pick", [P, GPH, P], F32R)
        xin = sb("xin", [P, 2, TB, F])
        hT = sb("hT", [P, FH, N])
        kS = sb("kS", [P, H, N], F32R)
        v_sb = sb("v_sb", [P, BLK, F])
        stats = sb("stats", [P, TB, 6])
        mv = sb("mv", [P, TB, 2])
        var = sb("var", [P, TB])
        rs = sb("rs", [P, BLK])
        nmr = sb("nmr", [P, BLK])
        tmp = sb("tmp", [P, TB])
        qM = sb("qM", [P, 2, 2, H, TW], F32R)
        e_sb = sb("e_sb", [P, ES, 2, TW])
        num = sb("num", [P, NS, TW])
        r_f = sb("r_f", [P, TW])
        r_hi = sb("r_hi", [P, TW], F32R)
        r_s = sb("r_s", [P, TW], F32R)
        ctxT = sb("ctxT", [P, PAIRS, TW])
        xr = sb("xr", [P, TB, F])
        hy = sb("hy", [P, TB, F])
        st2 = sb("st2", [P, TB, 6])
        mv2 = sb("mv2", [P, TB, 2])
        rs2 = sb("rs2", [P, TB])
        tmp2 = sb("tmp2", [P, TB])
        var2 = sb("var2", [P, TB])
        credit = sb("credit", [P, 1])

        psS = ps("psS", [P, 2, 2, TW])
        psN = ps("psN", [P, PAIRS, TW])
        psD = ps("psD", [P, TW])
        psM = ps("psM", [P, TW])

        const_in = sem("const_in")
        adj_in = [sem(f"adj_in{i}") for i in range(2)]
        mask_done = [sem(f"mask_done{i}") for i in range(2)]
        ident_done = sem("ident_done")
        consts_done = sem("consts_done")
        pool_chain = sem("pool_chain")
        x_in = [sem(f"x_in{i}") for i in range(2)]
        ln_chain, ln2_chain = sem("ln_chain"), sem("ln2_chain")
        stats_done = sem("stats_done")
        h_done = sem("h_done")
        tr_done = sem("tr_done")
        hT_done = sem("hT_done")
        kproj_done = sem("kproj_done")
        khi_done = sem("khi_done")
        klo_done = sem("klo_done")
        vproj_done = sem("vproj_done")
        v_done = sem("v_done")
        qproj_done = sem("qproj_done")
        qhi_done = sem("qhi_done")
        qlo_done = sem("qlo_done")
        scores_done = sem("scores_done")
        clip_done = sem("clip_done")
        exp_done = sem("exp_done")
        num_done = sem("num_done")
        numcopy_done = sem("numcopy_done")
        sums_done = sem("sums_done")
        sums_read = sem("sums_read")
        inv_done = sem("inv_done")
        inv_hi_done = sem("inv_hi_done")
        r_done = sem("r_done")
        bcast_done = sem("bcast_done")
        norm_done = sem("norm_done")
        ctx_done = sem("ctx_done")
        oproj_done = sem("oproj_done")
        xr_in = sem("xr_in")
        hr_done = sem("hr_done")
        hb_done = sem("hb_done")
        y_done = sem("y_done")
        yn_done = sem("yn_done")
        affine_chain = sem("affine_chain")
        o_done = sem("o_done")
        x1_out = sem("x1_out")

        stage = [e_sb[:, 0:4, :, :].rearrange("p s a w -> p (s a) w").bitcast(I32), num[:, 0:8, :].bitcast(I32)]
        adj_v = adjT.rearrange("(k p) n -> p k n", p=P)
        x_v = x.rearrange("b (t j p) f -> b t p j f", p=P, j=TB)
        x1_v = x1.rearrange("b (t j p) f -> b t p j f", p=P, j=TB)
        HALVES = 2 * T
        GROUPS = HALVES * GPH
        SUMS = T * (2 * GPH - PAIRS)

        def sums_until(half, i):
            if half % 2 == 0:
                return half * GPH - half // 2 * PAIRS + max(i, i % PAIRS + PAIRS) + 1 - PAIRS
            return half * GPH - (half + 1) // 2 * PAIRS + i + 1

        def place(s):
            return s % STEPS // SPC * KPC + s % KPC, s // KPC % PAIRS

        def chunk_sums_until(s):
            return s // SPC * KPC + s % KPC + 1

        def later_stage(s):
            half, tile = s // HALF - 1, (s - HALF) // STEPS - 1
            return (half if 0 <= half < HALVES else None, s % HALF,
                    tile if 0 <= tile < T else None, (s - HALF) % STEPS)

        def next_query(s):
            t = s // STEPS + 1
            return (t if t < T and s % STEPS < HALF else None), s % STEPS

        def tile_of(v, b, t):
            return v[bass.ds(b, 1), t:t + 1].rearrange("o q p j f -> (o q p) j f")

        block = ctx.enter_context(nc.Block())

        @block.sync
        def _(sp):
            def load_x(b, t, first=False):
                if not (first and t < 2):
                    sp.wait_ge(tr_done, b * T + t - 1)
                sp.dma_start(xin[:, t % 2], tile_of(x_v, b, t)).then_inc(x_in[t % 2], 16)

            def load_adjacency(t):
                for k in range(2):
                    if t >= 1:
                        sp.wait_ge(mask_done[k], t)
                    sp.dma_start(stage[k], adj_v[:, 8 * k:8 * k + 8, t * TW:(t + 1) * TW]).then_inc(adj_in[k], 16)

            def load_residual(b, t):
                sp.wait_ge(x1_out, b * (16 * T) + 16 * t + 16)
                sp.dma_start(xr[:, :, :], tile_of(x_v, b, t)).then_inc(xr_in, 16)

            def store(b, t):
                sp.wait_ge(o_done, b * T + t + 1)
                sp.dma_start(tile_of(x1_v, b, t), hy[:, :, :]).then_inc(x1_out, 16)

            def batch(b, last):
                if not last:
                    load_x(b + 1, 0)
                    load_x(b + 1, 1)
                for t in range(T - 1):
                    load_residual(b, t)
                    store(b, t)
                load_residual(b, T - 1)
                if not last:
                    load_x(b + 1, 2)
                    load_x(b + 1, 3)
                store(b, T - 1)

            load_x(0, 0, True)
            load_x(0, 1, True)
            for dst, src in ((w_k, wkT), (w_v, wvT), (w_q, wqT), (w_o, woT)):
                sp.dma_start(dst[:, :, :], src.rearrange("(c p) n -> p c n", p=P)).then_inc(const_in, 16)
            sp.dma_start(b_q[:, :], bq).then_inc(const_in, 16)
            sp.dma_start(b_k[:, :], bk).then_inc(const_in, 16)
            for dst, src in ((b_v, bv), (b_o, bo), (g_row, gamma), (be_row, beta)):
                sp.dma_start(dst[:, :], src.partition_broadcast(P)).then_inc(const_in, 16)
            load_adjacency(0)
            load_x(0, 2, True)
            load_adjacency(1)
            load_x(0, 3, True)
            load_adjacency(2)
            load_adjacency(3)
            if nb > 1:
                with sp.Fori(0, nb - 1) as b:
                    batch(b, False)
            batch(nb - 1, True)
            sp.wait_ge(x1_out, nb * T * 16 + 16)

        @block.gpsimd
        def _(pool):
            count = [0]

            def chain(ins):
                count[0] += 1
                ins.then_inc(pool_chain, 1)
                pool.wait_ge(pool_chain, count[0])

            pool.memset(credit[:, :], 0.0).then_inc(x1_out, 16)
            chain(pool.memset(ident[:, :], 0.0))
            pool.affine_select(out=ident[:, :], in_=ident[:, :], compare_op=ALU.not_equal, fill=1.0,
                               base=0, pattern=[[-1, P]], channel_multiplier=1).then_inc(ident_done, 1)
            chain(pool.memset(hot[:, :, :], 0.0))
            for c in range(CPH):
                chain(pool.memset(hot[:, c, :].rearrange("p (a r) -> p a r", r=CPH)[:, :, c], 1.0))
            chain(pool.memset(lo_rows[:, :], 0.0))
            for q in range(H):
                for c in range(CPH):
                    chain(pool.affine_select(out=lo_rows[:, :], in_=lo_rows[:, :], compare_op=ALU.not_equal,
                                             fill=-1.0, base=-(32 * q + CPH + c), pattern=[[0, 1]],
                                             channel_multiplier=1))
            for g in range(GPH):
                c, pair = g // PAIRS, g % PAIRS
                chain(pool.memset(pick_f[:, :], 0.0))
                for i in range(2):
                    for part in range(2):
                        row = 32 * (2 * pair + i) + CPH * part + c
                        chain(pool.affine_select(out=pick_f[:, 64 * i:64 * i + 64],
                                                 in_=pick_f[:, 64 * i:64 * i + 64],
                                                 compare_op=ALU.not_equal, fill=1.0, base=-row,
                                                 pattern=[[0, 64]], channel_multiplier=1))
                ins = pool.tensor_copy(pick[:, g, :], pick_f[:, :])
                if g < GPH - 1:
                    chain(ins)
            ins.then_inc(consts_done, 1)
            pool.wait_ge(const_in, 16 * NCONST)

            def step(b, s):
                half, ss, t, st = later_stage(s)
                i = ss - PICK_AT - 1
                if half is not None and 0 <= i < GPH:
                    pair, slot = i % PAIRS, (half * GPH + i) % NS
                    if half % 2 == 0 and i < 2 * PAIRS:
                        if i >= PAIRS:
                            pool.wait_ge(norm_done, b * GROUPS + half * GPH + i + 1)
                            if half >= 2:
                                pool.wait_ge(oproj_done, b * (2 * T) + half)
                            pool.tensor_tensor(ctxT[:, pair, :], num[:, (slot - PAIRS) % NS, :], num[:, slot, :],
                                               ALU.add).then_inc(ctx_done, 1)
                    else:
                        pool.wait_ge(norm_done, b * GROUPS + half * GPH + i + 1)
                        before = (half, i - PAIRS) if i >= PAIRS else (half - 1, GPH + i - PAIRS)
                        pool.wait_ge(ctx_done, b * SUMS + sums_until(*before))
                        pool.tensor_tensor(ctxT[:, pair, :], ctxT[:, pair, :], num[:, slot, :], ALU.add)                            .then_inc(ctx_done, 1)
                if half is not None and half % 2 == 1 and ss == 1:
                    pool.wait_ge(hr_done, b * T + half // 2 + 1)
                    pool.tensor_tensor(hy[:, :, :], hy[:, :, :], b_o[:, None, :].to_broadcast([P, TB, F]),
                                       ALU.add).then_inc(hb_done, 1)
                if t is not None and st == LN_AT + 3:
                    pool.wait_ge(yn_done, b * T + t + 1)
                    pool.tensor_tensor(hy[:, :, :], hy[:, :, :], g_row[:, None, :].to_broadcast([P, TB, F]),
                                       ALU.mult).then_inc(affine_chain, 1)
                    pool.wait_ge(affine_chain, b * (2 * T) + 2 * t + 1)
                    pool.wait_ge(xr_in, b * (16 * T) + 16 * t + 16)
                    pool.tensor_tensor(hy[:, :, :], hy[:, :, :], xr[:, :, :], ALU.add).then_inc(affine_chain, 1)
                    pool.wait_ge(affine_chain, b * (2 * T) + 2 * t + 2)
                    pool.tensor_tensor(hy[:, :, :], hy[:, :, :], be_row[:, None, :].to_broadcast([P, TB, F]),
                                       ALU.add).then_inc(o_done, 1)

            with pool.Fori(0, nb) as b:
                for s in range(HALF, BSTEPS + TAIL):
                    step(b, s)

        @block.scalar
        def _(act):
            def q_high(b, t, pair):
                act.wait_ge(qproj_done, b * (T * PAIRS) + t * PAIRS + pair + 1)
                for i in range(2):
                    rows = slice(64 * i, 64 * i + 64)
                    for j in range(2):
                        ins = act.activation(qM[64 * j:64 * j + 64, t % 2, 0, 2 * pair + i, :], psM[rows, :],
                                             ACT.Identity, bias=b_q[rows, pair:pair + 1])
                ins.then_inc(qhi_done, 1)

            def prepare(b, v):
                for t in range(T):
                    if v == H_AT[t]:
                        act.wait_ge(stats_done, b * T + t + 1)
                        for j in range(TB):
                            n = TB * t + j
                            ins = act.activation(xin[:, t % 2, j, :], xin[:, t % 2, j, :], ACT.Relu,
                                                 bias=nmr[:, n:n + 1], scale=rs[:, n:n + 1])
                        ins.then_inc(h_done, 1)
                    if v == TR_AT[t] + 1:
                        act.wait_ge(tr_done, b * T + t + 1)
                        act.activation(hT[:, 1, t * TW:(t + 1) * TW], psS[:, 0, 1, :], ACT.Copy).then_inc(hT_done, 1)
                    pair = v - TR_AT[t] - 2
                    if 0 <= pair < PAIRS:
                        act.wait_ge(kproj_done, b * (T * PAIRS) + t * PAIRS + pair + 1)
                        for i in range(2):
                            rows = slice(64 * i, 64 * i + 64)
                            ins = act.activation(kS[rows, 2 * pair + i, t * TW:(t + 1) * TW],
                                                 psS[rows, 1, pair, :], ACT.Identity,
                                                 bias=b_k[rows, pair:pair + 1])
                        ins.then_inc(khi_done, 1)
                pair = v - Q_AT
                if 0 <= pair < PAIRS:
                    q_high(b, 0, pair)

            def step(b, s):
                half, ss, _, _ = later_stage(s)
                if s >= 2 * LAG and s % 2 == 0 and s < BSTEPS + 2 * LAG:
                    g = s // 2 - LAG
                    act.wait_ge(num_done, b * GROUPS + g + 1)
                    if g >= NS:
                        act.wait_ge(ctx_done, b * SUMS + sums_until((g - NS) // GPH, (g - NS) % GPH))
                    act.activation(num[:, g % NS, :], psN[:, g % PAIRS, :], ACT.Copy).then_inc(numcopy_done, 1)
                if half is not None and ss == SUMS_AT:
                    act.wait_ge(sums_done, b * (BSTEPS // 2) + (half + 1) * CPH * KPC)
                    if half >= 1:
                        act.wait_ge(r_done, b * HALVES + half)
                    act.activation(r_f[:, :], psD[:, :], ACT.Copy).then_inc(sums_read, 1)
                if half is not None and ss == SPLIT_AT:
                    act.wait_ge(inv_done, b * HALVES + half + 1)
                    act.activation(r_hi[:, :], r_f[:, :], ACT.Copy).then_inc(inv_hi_done, 1)
                if s < BSTEPS:
                    act.wait_ge(clip_done, b * BSTEPS + s + 1)
                    act.activation(e_sb[:, s % ES], e_sb[:, s % ES], ACT.Exp, scale=SCALE).then_inc(exp_done, 1)
                if half is not None and half % 2 == 1 and ss == 0:
                    t = half // 2
                    act.wait_ge(xr_in, b * (16 * T) + 16 * t + 16)
                    for j in range(TB):
                        n = TB * t + j
                        ins = act.activation(hy[:, j, :], xr[:, j, :], ACT.Relu, bias=nmr[:, n:n + 1],
                                             scale=rs[:, n:n + 1])
                    ins.then_inc(hr_done, 1)
                t, st = next_query(s)
                if t is not None and st in (PROJ_AT, PROJ_AT + 2):
                    q_high(b, t, (st - PROJ_AT) // 2)

            act.wait_ge(const_in, 16 * NCONST)
            for v in range(-HALF, TAIL):
                prepare(0, v)
                if v in H_AT:
                    t = H_AT.index(v)
                    act.wait_ge(adj_in[1], 16 * (t + 1))
                    act.activation(mask[:, 8:16, t * TW:(t + 1) * TW], stage[1], ACT.Copy,
                                   bias=-CLIP_RAW, scale=2 * CLIP_RAW).then_inc(mask_done[1], 1)
            act.wait_ge(mask_done[0], T)
            act.wait_ge(mask_done[1], T)
            if nb > 1:
                with act.Fori(0, nb - 1) as b:
                    for s in range(BSTEPS + TAIL):
                        step(b, s)
                        prepare(b + 1, s - BSTEPS)
            for s in range(BSTEPS + TAIL):
                step(nb - 1, s)

        @block.vector
        def _(dve):
            def q_low(b, t, pair):
                dve.wait_ge(qhi_done, b * (T * PAIRS) + t * PAIRS + pair + 1)
                for i in range(2):
                    rows = slice(64 * i, 64 * i + 64)
                    hd = 2 * pair + i
                    for j in range(2):
                        ins = dve.scalar_tensor_tensor(
                            out=qM[64 * j:64 * j + 64, t % 2, 1, hd, :], in0=psM[rows, :],
                            scalar=b_q[rows, pair:pair + 1], in1=qM[rows, t % 2, 0, hd, :].bitcast(F32),
                            op0=ALU.add, op1=ALU.subtract)
                ins.then_inc(qlo_done, 1)

            def linker(chain, before):
                count = [0]

                def link(ins):
                    count[0] += 1
                    ins.then_inc(chain, 1)
                    dve.wait_ge(chain, before + count[0])
                return link

            def prepare(b, v, first):
                for t in range(T):
                    blocks = slice(TB * t, TB * t + TB)
                    if v == STATS_AT[t]:
                        link = linker(ln_chain, (b * T + t) * LN)
                        dve.wait_ge(x_in[t % 2], b * (8 * T) + 16 * (t // 2) + 16)
                        ln_moments(dve, link, mv, stats, var[:, :], lambda j: xin[:, t % 2, j, :], TB)
                        if t == T - 1 and not first:
                            dve.wait_ge(hr_done, b * T)
                        ln_rsqrt(dve, link, rs[:, blocks], tmp[:, :], var[:, :], mv)
                        dve.scalar_tensor_tensor(out=nmr[:, blocks], in0=mv[:, :, 0], scalar=-1.0, in1=rs[:, blocks],
                                                 op0=ALU.mult, op1=ALU.mult).then_inc(stats_done, 1)
                    if v == TR_AT[t] + 1:
                        dve.wait_ge(tr_done, b * T + t + 1)
                        dve.tensor_copy(hT[:, 0, t * TW:(t + 1) * TW], psS[:, 0, 0, :]).then_inc(hT_done, 1)
                    pair = v - TR_AT[t] - 2
                    if 0 <= pair < PAIRS:
                        dve.wait_ge(khi_done, b * (T * PAIRS) + t * PAIRS + pair + 1)
                        for i in range(2):
                            rows = slice(64 * i, 64 * i + 64)
                            other = slice(64 - 64 * i, 128 - 64 * i)
                            cols = slice(t * TW, (t + 1) * TW)
                            ins = dve.scalar_tensor_tensor(
                                out=kS[other, 2 * pair + i, cols], in0=psS[rows, 1, pair, :],
                                scalar=b_k[rows, pair:pair + 1],
                                in1=kS[rows, 2 * pair + i, cols].bitcast(F32),
                                op0=ALU.add, op1=ALU.subtract)
                        ins.then_inc(klo_done, 1)
                    j = v - TR_AT[t] - 2 - PAIRS
                    if 0 <= j < TB // 2:
                        n = TB * t + 2 * j
                        dve.wait_ge(vproj_done, b * (BLK // 2) + n // 2 + 1)
                        dve.tensor_tensor(v_sb[:, n:n + 2, :],
                                          psN[:, j, :].rearrange("p (a f) -> p a f", a=2),
                                          b_v[:, None, :].to_broadcast([P, 2, F]), ALU.add).then_inc(v_done, 1)
                pair = v - Q_AT
                if 0 <= pair < PAIRS:
                    q_low(b, 0, pair)

            def step(b, s):
                half, ss, t, st = later_stage(s)
                i = ss - PICK_AT - 1
                if half is not None and 0 <= i < GPH:
                    slot = (half * GPH + i) % NS
                    dve.wait_ge(bcast_done, b * GROUPS + half * GPH + i + 1)
                    dve.wait_ge(numcopy_done, b * GROUPS + half * GPH + i + 1)
                    dve.tensor_tensor(num[:, slot, :], num[:, slot, :], psM[:, :], ALU.mult).then_inc(norm_done, 1)
                if t is not None and st in (PROJ_AT + 1, PROJ_AT + 3):
                    j = (st - PROJ_AT) // 2
                    dve.wait_ge(oproj_done, b * (2 * T) + 2 * t + j + 1)
                    dve.wait_ge(hb_done, b * T + t + 1)
                    dve.tensor_tensor(hy[:, 2 * j:2 * j + 2, :], psM[:, :].rearrange("p (a f) -> p a f", a=2),
                                      hy[:, 2 * j:2 * j + 2, :], ALU.add).then_inc(y_done, 1)
                if s < BSTEPS:
                    kb, _ = place(s)
                    cols = slice(s // STEPS * TW, (s // STEPS + 1) * TW)
                    if s >= ES:
                        dve.wait_ge(sums_done, b * (BSTEPS // 2) + chunk_sums_until(s - ES))
                    dve.wait_ge(scores_done, b * BSTEPS + s + 1)
                    dve.scalar_tensor_tensor(
                        out=e_sb[:, s % ES], in0=psS[:, s % 2], scalar=-CLIP_RAW,
                        in1=mask[:, kb, cols][:, None, :].to_broadcast([P, 2, TW]),
                        op0=ALU.max, op1=ALU.min).then_inc(clip_done, 1)
                if half is not None and INV_AT <= ss < INV_AT + TB:
                    cols = slice((ss - INV_AT) * P, (ss - INV_AT + 1) * P)
                    if ss == INV_AT:
                        dve.wait_ge(sums_read, b * HALVES + half + 1)
                    ins = dve.reciprocal(r_f[:, cols], r_f[:, cols])
                    if ss == INV_AT + TB - 1:
                        ins.then_inc(inv_done, 1)
                if half is not None and ss == SPLIT_AT:
                    dve.wait_ge(inv_hi_done, b * HALVES + half + 1)
                    if half >= 1:
                        dve.wait_ge(bcast_done, b * GROUPS + half * GPH)
                    dve.scalar_tensor_tensor(out=r_s[:, :], in0=r_hi[:, :].bitcast(F32), scalar=lo_rows[:, 0:1],
                                             in1=r_f[:, :], op0=ALU.mult, op1=ALU.add).then_inc(r_done, 1)
                if t is not None and LN_AT <= st < LN_AT + 3:
                    n = b * T + t
                    if st == LN_AT:
                        dve.wait_ge(y_done, 2 * n + 2)
                        ln_moments(dve, linker(ln2_chain, n * LN), mv2, st2, var2[:, :], lambda j: hy[:, j, :], TB)
                    if st == LN_AT + 1:
                        ln_rsqrt(dve, linker(ln2_chain, n * LN + 2), rs2[:, :], tmp2[:, :], var2[:, :], mv2)
                    if st == LN_AT + 2:
                        for j in range(TB):
                            ins = dve.tensor_scalar(hy[:, j, :], hy[:, j, :], mv2[:, j, 0:1], rs2[:, j:j + 1],
                                                    ALU.subtract, ALU.mult)
                        ins.then_inc(yn_done, 1)
                t, st = next_query(s)
                if t is not None and st in (PROJ_AT, PROJ_AT + 2):
                    q_low(b, t, (st - PROJ_AT) // 2)

            for v in range(-HALF, TAIL):
                if v == H_AT[0]:
                    dve.wait_ge(const_in, 16 * NCONST)
                prepare(0, v, True)
                if v in STATS_AT:
                    t = STATS_AT.index(v)
                    dve.wait_ge(adj_in[0], 16 * (t + 1))
                    dve.tensor_scalar(mask[:, 0:8, t * TW:(t + 1) * TW], stage[0], 2 * CLIP_RAW, -CLIP_RAW,
                                      ALU.mult, ALU.add).then_inc(mask_done[0], 1)
            dve.wait_ge(consts_done, 1)
            dve.wait_ge(mask_done[0], T)
            dve.wait_ge(mask_done[1], T)
            if nb > 1:
                with dve.Fori(0, nb - 1) as b:
                    for s in range(BSTEPS + TAIL):
                        step(b, s)
                        prepare(b + 1, s - BSTEPS, False)
            for s in range(BSTEPS + TAIL):
                step(nb - 1, s)

        @block.tensor
        def _(pe):
            def q_proj(b, t, pair):
                for c in range(FH):
                    ins = pe.matmul(psM[:, :], w_q[:, c, pair * P:(pair + 1) * P],
                                    hT[:, c, t * TW:(t + 1) * TW], start=c == 0, stop=c == FH - 1)
                ins.then_inc(qproj_done, 1)

            def prepare(b, v, first):
                for t in range(T):
                    cols = slice(t * TW, (t + 1) * TW)
                    if v == TR_AT[t]:
                        pe.wait_ge(h_done, b * T + t + 1)
                        if t:
                            pe.wait_ge(hT_done, b * (2 * T) + 2 * t)
                        elif not first:
                            pe.wait_ge(clip_done, b * BSTEPS)
                        for c in range(FH):
                            for j in range(TB):
                                ins = pe.transpose(psS[:, 0, c, j * P:(j + 1) * P],
                                                   xin[:, t % 2, j, c * P:(c + 1) * P], ident[:, :])
                        ins.then_inc(tr_done, 1)
                    pair = v - TR_AT[t] - 1
                    if 0 <= pair < PAIRS:
                        if pair == 0:
                            pe.wait_ge(hT_done, b * (2 * T) + 2 * t + 2)
                        if t:
                            pe.wait_ge(klo_done, b * (T * PAIRS) + (t - 1) * PAIRS + pair + 1)
                        for c in range(FH):
                            ins = pe.matmul(psS[:, 1, pair, :], w_k[:, c, pair * P:(pair + 1) * P],
                                            hT[:, c, cols], start=c == 0, stop=c == FH - 1)
                        ins.then_inc(kproj_done, 1)
                    j = v - TR_AT[t] - 1 - PAIRS
                    if 0 <= j < TB // 2:
                        n = TB * t + 2 * j
                        if t:
                            pe.wait_ge(v_done, b * (BLK // 2) + n // 2 - 1)
                        elif not first:
                            pe.wait_ge(numcopy_done, b * GROUPS)
                        for a in range(2):
                            for c in range(FH):
                                ins = pe.matmul(psN[:, j, a * F:(a + 1) * F],
                                                hT[:, c, (n + a) * P:(n + a + 1) * P], w_v[:, c, :],
                                                start=c == 0, stop=c == FH - 1)
                        ins.then_inc(vproj_done, 1)
                pair = v - Q_AT
                if 0 <= pair < PAIRS:
                    if pair:
                        pe.wait_ge(qlo_done, b * (T * PAIRS) + pair)
                    elif not first:
                        pe.wait_ge(y_done, b * (2 * T))
                    q_proj(b, 0, pair)
                if v == TAIL - 1:
                    pe.wait_ge(klo_done, b * (T * PAIRS) + T * PAIRS)
                    pe.wait_ge(v_done, b * (BLK // 2) + BLK // 2)

            def step(b, s):
                if s < BSTEPS:
                    t, (kb, pair) = s // STEPS, place(s)
                    if s >= 2:
                        pe.wait_ge(clip_done, b * BSTEPS + s - 1)
                    if s % STEPS in (0, KPC):
                        pe.wait_ge(qlo_done, b * (T * PAIRS) + t * PAIRS + pair + 1)
                    for i in range(2):
                        hd = 2 * pair + i
                        for part in range(2):
                            ins = pe.matmul(psS[:, s % 2, i, :], kS[:, hd, kb * P:(kb + 1) * P],
                                            qM[:, t % 2, part, hd, :], start=part == 0, stop=part == 1)
                    ins.then_inc(scores_done, 1)
                u = s - LAG
                if 0 <= u < BSTEPS:
                    (kb, pair), g = place(u), u // KPC
                    pe.wait_ge(exp_done, b * BSTEPS + u + 1)
                    if u % KPC == 0 and g >= PAIRS:
                        pe.wait_ge(numcopy_done, b * GROUPS + g - 1)
                    for i in range(2):
                        hd = 2 * pair + i
                        ins = pe.matmul(psN[64 * i:64 * i + 64, pair, :], v_sb[:, kb, hd * D:(hd + 1) * D],
                                        e_sb[:, u % ES, i, :], start=u % KPC == 0, stop=u % KPC == KPC - 1,
                                        skip_group_check=True)
                    if u % KPC == KPC - 1:
                        ins.then_inc(num_done, 1)
                    if pair == PAIRS - 1:
                        c = u // SPC % CPH
                        first, last = u % HALF == KPC, u % HALF == HALF - 1
                        if first and u >= HALF:
                            pe.wait_ge(sums_read, b * HALVES + u // HALF)
                        for hd in range(H):
                            slot = (u - KPC * (PAIRS - 1 - hd // 2)) % ES
                            ins = pe.matmul(psD[32 * hd:32 * hd + 32, :], hot[:, c, :],
                                            e_sb[:, slot, hd % 2, :], start=first, stop=last,
                                            skip_group_check=True)
                        ins.then_inc(sums_done, 1)
                half, ss, t, st = later_stage(s)
                i = ss - PICK_AT
                if half is not None and 0 <= i < GPH:
                    n = half * GPH + i
                    if i == 0:
                        pe.wait_ge(r_done, b * HALVES + half + 1)
                    else:
                        pe.wait_ge(norm_done, b * GROUPS + n)
                    pe.matmul(psM[:, :], pick[:, i, :], r_s[:, :], start=True, stop=True).then_inc(bcast_done, 1)
                if t is not None and st in (PROJ_AT, PROJ_AT + 2):
                    j = (st - PROJ_AT) // 2
                    if j == 0:
                        pe.wait_ge(ctx_done, b * SUMS + sums_until(2 * t + 1, GPH - 1))
                    else:
                        pe.wait_ge(y_done, b * (2 * T) + 2 * t + 1)
                    for a in range(2):
                        col = (2 * j + a) * P
                        for pair in range(PAIRS):
                            ins = pe.matmul(psM[:, a * F:(a + 1) * F], ctxT[:, pair, col:col + P],
                                            w_o[:, pair, :], start=pair == 0, stop=pair == PAIRS - 1)
                    ins.then_inc(oproj_done, 1)
                t, st = next_query(s)
                if t is not None and st in (PROJ_AT - 1, PROJ_AT + 1):
                    pair = (st - PROJ_AT + 1) // 2
                    if pair or t == 1:
                        pe.wait_ge(qlo_done, b * (T * PAIRS) + t * PAIRS + pair)
                    else:
                        pe.wait_ge(norm_done, b * GROUPS + (s // HALF - 1) * GPH)
                    q_proj(b, t, pair)

            pe.wait_ge(ident_done, 1)
            pe.wait_ge(const_in, 16 * NCONST)
            for v in range(TAIL):
                prepare(0, v, True)
            pe.wait_ge(consts_done, 1)
            if nb > 1:
                with pe.Fori(0, nb - 1) as b:
                    for s in range(BSTEPS + TAIL):
                        step(b, s)
                        prepare(b + 1, s - BSTEPS, False)
            for s in range(BSTEPS + TAIL):
                step(nb - 1, s)


W1 = D + 2
XW = D + 1
PARTS = 3
KC = 4
KCH = BLK // KC
U = H * T
SLOTS = U * KCH
ROT = 2 * KCH
ALPHA = 0.2
BIG = 2.0 ** 60
SHIFT = 60.0
EI_ROWS = (0, 64, 96)
LN_W = (10, 15, 20, 25)
WH_W = 32
MAX_W = WH_W + BLK
EIP_W = 58
XY_W = ((MAX_W + 6, MAX_W + 8, MAX_W + 10, MAX_W + 11), (2, 4, 5, 6), (14, 19, 20, 21), (28, 36, 37, 38))
ELU_W = SLOTS - 2
ELU2_W = 6


def layer1(nc, mask, x1, w, a1, a2, out, nb):
    with ExitStack() as ctx:
        def sb(name, shape, dt=F32):
            return ctx.enter_context(nc.sbuf_tensor(name, shape, dt))

        def ps(name, shape, dt=F32):
            return ctx.enter_context(nc.psum_tensor(name, shape, dt))

        def sem(name):
            return ctx.enter_context(nc.semaphore(name))

        adj = sb("adj", [P, BLK, N], BF16)
        w_all = sb("w_all", [P, FH, H, W1])
        w_ei = sb("w_ei", [P, FH, P])
        sel = sb("sel", [P, H, P], BF16)
        ident = sb("ident1", [P, P])
        ones = sb("ones1", [H, P])
        xin = sb("xin1", [P, 2, TB, F])
        stats = sb("stats1", [P, TB, 6])
        mv = sb("mv1", [P, TB, 2])
        rs = sb("rs1", [P, 2, TB])
        nmr = sb("nmr1", [P, 2, TB])
        var = sb("var1", [P, TB])
        tmp = sb("tmp1", [P, TB])
        hT = sb("hT1", [P, FH, N])
        wh = sb("wh", [P, BLK, H, W1])
        mx_p = sb("mx_p", [P, H])
        mx = sb("mx", [H, 1])
        mx_d = sb("mx_d", [H, H])
        cen = sb("cen", [P, H])
        xq = sb("xq", [P, 2, BLK, H])
        cq, cq_n = sb("cq", [P, 2, BLK, H]), sb("cq_n", [P, 2, BLK, H])
        bigj, bigj_n = sb("bigj", [P, BLK, H]), sb("bigj_n", [P, BLK, H])
        eip, eip_n = sb("eip", [P, N], BF16), sb("eip_n", [P, N], BF16)
        ei_f = sb("ei_f", [P, TW])
        xf = sb("xf", [P, 2, BLK, XW])
        xy = sb("xy", [P, 2, 2, BLK, PARTS, XW], BF16)
        pos, neg = (mask[:, 8 * i:8 * i + 8, :].rearrange("p k n -> p (k n)").bitcast(BF16)
                    .rearrange("p (c k n) -> p c k n", c=KCH, k=KC) for i in range(2))
        red = sb("red", [P, 2, TB, 2, XW])
        rden = sb("rden", [P, 2, TB])
        o_sb = sb("o_sb", [P, BLK, F])
        em = sb("em", [P, 2, TB, F])
        xo = sb("xo", [P, TB, F])

        psP = ps("psP", [P, 2, TW])
        psE = ps("psE", [P, 2, TW])
        psA = ps("psA", [P, TB, TW])

        const_in = sem("const1_in")
        adj_done = sem("adj1_done")
        ident_done = sem("ident1_done")
        sel_f_done = sem("sel_f_done")
        sel_done = sem("sel_done")
        w_chain = sem("w1_chain")
        w_done = sem("w1_done")
        x_in = [sem(f"x1_in{i}") for i in range(2)]
        ln_chain = sem("ln1_chain")
        stats_done = sem("stats1_done")
        h_done = sem("h1_done")
        tr_done = sem("tr1_done")
        hT_done = sem("hT1_done")
        eiT_done = sem("eiT_done")
        ei_hi_done = sem("ei_hi_done")
        ei_rest_done = sem("ei_rest_done")
        ei_mid_done = sem("ei_mid_done")
        ei_lo_done = sem("ei_lo_done")
        eip_done = sem("eip_done")
        wh_proj = sem("wh_proj")
        wh_done = [sem(f"wh_done{i}") for i in range(2)]
        mx_chain = sem("mx_chain")
        mx_part = sem("mx_part")
        mx_turned = sem("mx_turned")
        mx_diag = sem("mx_diag")
        mx_done = sem("mx_done")
        d_done = sem("d_done")
        q_done = sem("q_done")
        cq_done = sem("cq_done")
        bigj_done = sem("bigj_done")
        xf_done = sem("xf_done")
        hi_done = sem("hi1_done")
        rest_done = sem("rest_done")
        mid_done = sem("mid_done")
        xy_done = sem("xy_done")
        ei_done = sem("ei_done")
        step_done = sem("step_done")
        pos_done = sem("pos_done")
        neg_done = sem("neg_done")
        piece_free = sem("piece_free")
        acc_done = sem("acc_done")
        red_done = sem("red_done")
        mix_chain = sem("mix_chain")
        mix_done = sem("mix_done")
        rden_done = sem("rden_done")
        o_done = sem("o1_done")
        xo_in = sem("xo_in")
        xo_used = sem("xo_used")
        minus_done = sem("minus_done")
        en_done = sem("en_done")
        relu_done = sem("relu_done")
        fin_done = sem("fin_done")
        out_done = [sem(f"out_done{t}") for t in range(T)]

        x_v = x1.rearrange("b (t j p) f -> b t p j f", p=P, j=TB)
        out_v = out.rearrange("b (t j p) f -> b t p j f", p=P, j=TB)

        def tile_of(v, b, t):
            return v[bass.ds(b, 1), t:t + 1].rearrange("o q p j f -> (o q p) j f")

        def run(engine, work, prepare, lag=0):
            for s in range(SLOTS):
                prepare(0, s, True)
            for s in range(ROT):
                work(0, s, first=True, last=nb == 1)
            if nb > 1:
                with engine.Fori(0, nb - 1) as b:
                    for s in range(ROT, SLOTS):
                        work(b, s, first=False, last=False)
                        prepare(b + 1, s + lag, False)
                    for s in range(ROT):
                        work(b + 1, s, first=False, last=False)
            for s in range(ROT, SLOTS + ROT):
                work(nb - 1, s, first=False, last=True)

        block = ctx.enter_context(nc.Block())

        @block.sync
        def _(sp):
            def load_x(b, t, first):
                if not (first and t < 2):
                    sp.wait_ge(tr_done, b * T + t - 1)
                sp.dma_start(xin[:, t % 2], tile_of(x_v, b, t)).then_inc(x_in[t % 2], 16)

            def load_xo(b, t):
                sp.wait_ge(xo_used, b * T + t + 1)
                sp.dma_start(xo[:, :, :], tile_of(x_v, b, t)).then_inc(xo_in, 16)

            def batch(b, last):
                if not last:
                    for t in range(T):
                        load_x(b + 1, t, False)
                load_xo(b, 0)
                for t in range(T):
                    if t < T - 1:
                        load_xo(b, t + 1)
                    sp.wait_ge(fin_done, b * T + t + 1)
                    sp.dma_start(tile_of(out_v, b, t), o_sb[:, TB * t:TB * t + TB, :]).then_inc(out_done[t], 16)

            load_x(0, 0, True)
            for c in range(FH):
                sp.dma_start(w_all[:, c, :, 0:D], w[c * P:(c + 1) * P, :, :]).then_inc(const_in, 16)
            sp.dma_start(xf[:, 0, 0:H, 0:D], a1.partition_broadcast(P)).then_inc(const_in, 16)
            sp.dma_start(xf[:, 0, H:2 * H, 0:D], a2.partition_broadcast(P)).then_inc(const_in, 16)
            for t in range(1, T):
                load_x(0, t, True)
            if nb > 1:
                with sp.Fori(0, nb - 1) as b:
                    batch(b, False)
            batch(nb - 1, True)
            for t in range(T):
                sp.wait_ge(out_done[t], nb * 16 + 16)

        @block.gpsimd
        def _(pool):
            def mix(b, u):
                unit, hd, t = b * U + u, u // T, u % T
                r, blocks = red[:, u % 2], slice(TB * t, TB * t + TB)
                pool.wait_ge(red_done, unit * TB + 2 * TB)
                if u == 0:
                    pool.wait_ge(cq_done, b + 1)
                for br in range(2):
                    ins = pool.tensor_tensor(r[:, :, br, :], r[:, :, br, :],
                                             cq[:, br, blocks, hd][:, :, None].to_broadcast([P, TB, XW]), ALU.mult)
                ins.then_inc(mix_chain, 1)
                pool.wait_ge(mix_chain, unit + 1)
                pool.tensor_tensor(r[:, :, 0, :], r[:, :, 0, :], r[:, :, 1, :], ALU.add).then_inc(mix_done, 1)
                pool.wait_ge(rden_done, unit + 1)
                if hd == 0:
                    pool.wait_ge(out_done[t], b * 16 + 16)
                pool.tensor_tensor(o_sb[:, blocks, hd * D:(hd + 1) * D], r[:, :, 0, 0:D],
                                   rden[:, u % 2, :][:, :, None].to_broadcast([P, TB, D]), ALU.mult).then_inc(o_done, 1)

            def finish(b, t):
                rows = slice(TB * t, TB * t + TB)
                pool.wait_ge(en_done, b * T + t + 1)
                pool.wait_ge(xo_in, b * (16 * T) + 16 * t + 16)
                pool.tensor_tensor(em[:, t % 2], em[:, t % 2], xo[:, :, :], ALU.add).then_inc(xo_used, 1)
                pool.tensor_scalar(o_sb[:, rows, :], o_sb[:, rows, :], 0.0, -1.0, ALU.max, ALU.add)\
                    .then_inc(relu_done, 1)
                pool.wait_ge(relu_done, b * T + t + 1)
                pool.wait_ge(xo_used, b * T + t + 2)
                pool.tensor_tensor(o_sb[:, rows, :], o_sb[:, rows, :], em[:, t % 2], ALU.add).then_inc(fin_done, 1)

            def work(b, s, first, last):
                u = s // KCH
                if s % KCH == KCH - 1:
                    if u:
                        mix(b, u - 1) if u <= U else None
                    elif not first:
                        mix(b - 1, U - 1)
                ends(b, s, first, last)
                for hd in range(1, H):
                    weigh(b, s, hd, False)

            def ends(b, s, first, last):
                if s == SLOTS - 1:
                    finish(b, 0)
                before = None if s < ROT and first else (b, s - SLOTS) if s >= SLOTS else (b - 1, s)
                if before is not None and (s < ROT or s >= SLOTS):
                    for t, at in ((1, 1), (2, ELU2_W), (3, ELU2_W + 1)):
                        if before[1] == at:
                            finish(before[0], t)

            def weigh(b, s, hd, first):
                mult_at, split_at, _, _ = XY_W[hd]
                for br in range(2):
                    n = b * (2 * H) + 2 * hd + br
                    f, hi = xf[:, br], xy[:, hd % 2, br, :, 0, :]
                    if s == mult_at + br:
                        if hd == 0 and br == 0:
                            pool.wait_ge(q_done, b + 1)
                        if not (first and hd == 0):
                            pool.wait_ge(xy_done, n - 1)
                        pool.tensor_tensor(f[:, :, 0:D], wh[:, :, hd, 0:D],
                                           xq[:, br, :, hd][:, :, None].to_broadcast([P, BLK, D]), ALU.mult)
                        pool.tensor_copy(f[:, :, D:XW], xq[:, br, :, hd][:, :, None]).then_inc(xf_done, 1)
                    if s == split_at + br:
                        pool.wait_ge(hi_done, n + 1)
                        pool.tensor_tensor(f, f, hi, ALU.subtract).then_inc(rest_done, 1)

            def prepare(b, s, first):
                weigh(b, s, 0, first)

            pool.memset(ones[:, :], 1.0).then_inc(out_done[0], 16)
            for t in range(1, T):
                pool.memset(xo[:, t, 0:1], 0.0).then_inc(out_done[t], 16)
            pool.memset(ident[:, :], 0.0).then_inc(ident_done, 1)
            pool.wait_ge(ident_done, 1)
            pool.affine_select(out=ident[:, :], in_=ident[:, :], compare_op=ALU.not_equal, fill=1.0,
                               base=0, pattern=[[-1, P]], channel_multiplier=1).then_inc(ident_done, 1)
            sel_f = em[:, 0, 0:2, :].rearrange("p a f -> p (a f)")
            pool.memset(sel_f, 0.0).then_inc(sel_f_done, 1)
            n = 1
            for hd in range(H):
                for row in EI_ROWS:
                    pool.wait_ge(sel_f_done, n)
                    cols = sel_f[:, hd * P:(hd + 1) * P]
                    pool.affine_select(out=cols, in_=cols, compare_op=ALU.not_equal, fill=1.0, base=-(row + hd),
                                       pattern=[[0, P]], channel_multiplier=1).then_inc(sel_f_done, 1)
                    n += 1
            run(pool, work, prepare)

        @block.scalar
        def _(act):
            def steps(b, u, c):
                unit, hd = b * U + u, u // T
                if c == 0:
                    act.wait_ge(ei_done, unit + 1)
                if c < KCH - 1:
                    act.wait_ge(piece_free, unit * (KCH - 1) + c + 1)
                else:
                    act.wait_ge(acc_done, unit * TB + TB)
                for k in range(KC):
                    kb = KC * c + k
                    ins = act.activation(pos[:, c, k, :], psE[:, u % 2, :], ACT.Sigmoid,
                                         bias=bigj[:, kb, hd:hd + 1], scale=BIG)
                ins.then_inc(step_done, 1)

            def elu(b, tiles):
                for t in tiles:
                    act.wait_ge(o_done, b * U + (U - T + t) + 3)
                    if t >= 2:
                        act.wait_ge(fin_done, b * T + t - 1)
                    act.activation(em[:, t % 2], o_sb[:, TB * t:TB * t + TB, :], ACT.Relu, scale=-1.0)\
                       .then_inc(minus_done, 1)
                for t in tiles:
                    act.wait_ge(minus_done, b * T + t + 1)
                    act.activation(em[:, t % 2], em[:, t % 2], ACT.Exp, scale=-1.0).then_inc(en_done, 1)

            def work(b, s, first, last):
                if s < SLOTS:
                    if s == 0:
                        if not first:
                            act.wait_ge(step_done, b * SLOTS)
                        act.activation(bigj[:, :, :], bigj_n[:, :, :], ACT.Copy).then_inc(bigj_done, 1)
                        act.wait_ge(bigj_done, b + 1)
                    steps(b, s // KCH, s % KCH)
                if s == ELU_W:
                    elu(b, (0, 1))
                if s == ELU2_W and not first:
                    elu(b - 1, (2, 3))
                if s == SLOTS + ELU2_W:
                    elu(b, (2, 3))
                for hd in range(1, H):
                    split(b, s, hd, False)

            def split(b, s, hd, first):
                _, hi_at, mid_at, _ = XY_W[hd]
                for br in range(2):
                    n = b * (2 * H) + 2 * hd + br
                    if s == hi_at + br:
                        act.wait_ge(xf_done, n + 1)
                        if not (first and hd == 0):
                            act.wait_ge(acc_done, b * (U * TB) + (hd - 1) * T * TB + TB)
                        act.activation(xy[:, hd % 2, br, :, 0, :], xf[:, br], ACT.Copy).then_inc(hi_done, 1)
                    if s == mid_at + br:
                        act.wait_ge(rest_done, n + 1)
                        act.activation(xy[:, hd % 2, br, :, 1, :], xf[:, br], ACT.Copy).then_inc(mid_done, 1)

            def prepare(b, s, first):
                for t in range(T):
                    at, cols = s - LN_W[t], slice(t * TW, (t + 1) * TW)
                    if at == 2:
                        act.wait_ge(stats_done, b * T + t + 1)
                        for j in range(TB):
                            ins = act.activation(xin[:, t % 2, j, :], xin[:, t % 2, j, :], ACT.Relu,
                                                 bias=nmr[:, t % 2, j:j + 1], scale=rs[:, t % 2, j:j + 1])
                        ins.then_inc(h_done, 1)
                    if at == 4:
                        act.wait_ge(tr_done, b * T + t + 1)
                        act.activation(hT[:, 1, cols], psP[:, 1, :], ACT.Copy).then_inc(hT_done, 1)
                    if at == 6:
                        act.wait_ge(eiT_done, b * T + t + 1)
                        if t == 0 and not first:
                            act.wait_ge(eip_done, b)
                        act.activation(eip_n[:, cols], psP[:, 0, :], ACT.Copy).then_inc(ei_hi_done, 1)
                    if at == 7:
                        rows = slice(EI_ROWS[1], P)
                        act.wait_ge(ei_rest_done, b * T + t + 1)
                        act.activation(eip_n[rows, cols], ei_f[rows, :], ACT.Copy).then_inc(ei_mid_done, 1)
                n = s - WH_W - 1
                if 0 <= n < BLK and n % 2 == 0:
                    act.wait_ge(wh_proj, b * BLK + n + 1)
                    if n == 0 and not first:
                        act.wait_ge(xf_done, b * (2 * H))
                    act.activation(wh[:, n].rearrange("p h e -> p (h e)"), psP[:, 0, 0:H * W1], ACT.Copy)\
                       .then_inc(wh_done[0], 1)
                if s == MAX_W + 5:
                    act.wait_ge(d_done, b + 1)
                    act.activation(xq[:, 1], xq[:, 0], ACT.Exp, scale=ALPHA)
                    act.activation(xq[:, 0], xq[:, 0], ACT.Exp)
                    act.activation(cq_n[:, 0], cq_n[:, 0], ACT.Exp, scale=1.0 - ALPHA)
                    act.activation(cq_n[:, 1], cq_n[:, 1], ACT.Exp, scale=ALPHA - 1.0).then_inc(q_done, 1)
                split(b, s, 0, first)
                if first and LN_W[0] + 2 <= s < LN_W[0] + 2 + BLK // 2:
                    kb = s - LN_W[0] - 2
                    act.activation(adj[:, kb, :], mask[:, kb, :], ACT.Copy, bias=0.5, scale=0.5 / CLIP_RAW)\
                       .then_inc(adj_done, 1)
                if first and s == SLOTS - 1:
                    act.wait_ge(adj_done, BLK)

            act.wait_ge(sel_f_done, 1 + H * PARTS)
            act.activation(sel[:, :, :].rearrange("p h m -> p (h m)"), em[:, 0, 0:2, :].rearrange("p a f -> p (a f)"),
                           ACT.Copy).then_inc(sel_done, 1)
            run(act, work, prepare)

        @block.vector
        def _(dve):
            def linker(chain, before):
                count = [0]

                def link(ins):
                    count[0] += 1
                    ins.then_inc(chain, 1)
                    dve.wait_ge(chain, before + count[0])
                return link

            def piece(b, u, c):
                n = (b * U + u) * KCH + c
                edges = adj[:, KC * c:KC * c + KC, u % T * TW:(u % T + 1) * TW]
                dve.wait_ge(step_done, n + 1)
                dve.tensor_tensor(pos[:, c], pos[:, c], edges, ALU.mult).then_inc(pos_done, 1)
                dve.wait_ge(pos_done, n + 1)
                dve.tensor_tensor(neg[:, c], edges, pos[:, c], ALU.subtract).then_inc(neg_done, 1)

            def reduce(b, u):
                unit = b * U + u
                dve.wait_ge(o_done, unit + 1)
                for j in range(TB):
                    dve.wait_ge(acc_done, unit * TB + TB + j + 1)
                    dve.tensor_reduce(red[:, u % 2, j], psA[:, j, 0:2 * PARTS * XW].rearrange(
                        "p (r c e) -> p r e c", r=2, c=PARTS), AX.X, ALU.add).then_inc(red_done, 1)

            def invert(b, u):
                dve.wait_ge(mix_done, b * U + u + 1)
                dve.reciprocal(rden[:, u % 2, :], red[:, u % 2, :, 0, D]).then_inc(rden_done, 1)

            def work(b, s, first, last):
                u, c = s // KCH, s % KCH
                if c in (2, KCH - 1):
                    stage = reduce if c == 2 else invert
                    if 1 <= u <= U:
                        if c == 2:
                            reduce(b, u - 1)
                    elif u == 0 and not first:
                        if c == 2:
                            reduce(b - 1, U - 1)
                if s < SLOTS:
                    piece(b, u, c)
                if c == KCH - 1:
                    if 1 <= u <= U:
                        invert(b, u - 1)
                    elif u == 0 and not first:
                        invert(b - 1, U - 1)
                if s == 4:
                    if not first:
                        dve.wait_ge(mix_chain, b * U)
                    dve.wait_ge(q_done, b + 1)
                    dve.tensor_copy(cq[:, :, :, :], cq_n[:, :, :, :]).then_inc(cq_done, 1)
                for hd in range(1, H):
                    low(b, s, hd)

            def low(b, s, hd):
                for br in range(2):
                    if s == XY_W[hd][3] + br:
                        dve.wait_ge(mid_done, b * (2 * H) + 2 * hd + br + 1)
                        mid, lo = (xy[:, hd % 2, br, :, i, :] for i in (1, 2))
                        dve.tensor_tensor(lo, xf[:, br], mid, ALU.subtract).then_inc(xy_done, 1)

            def prepare(b, s, first):
                for t in range(T):
                    at, cols = s - LN_W[t], slice(t * TW, (t + 1) * TW)
                    n = b * T + t
                    if at == 0:
                        dve.wait_ge(x_in[t % 2], b * (8 * T) + 16 * (t // 2) + 16)
                        ln_moments(dve, linker(ln_chain, n * LN), mv, stats, var[:, :],
                                   lambda j: xin[:, t % 2, j, :], TB)
                    if at == 1:
                        ln_rsqrt(dve, linker(ln_chain, n * LN + 2), rs[:, t % 2], tmp[:, :], var[:, :], mv)
                        dve.scalar_tensor_tensor(out=nmr[:, t % 2], in0=mv[:, :, 0], scalar=-1.0, in1=rs[:, t % 2],
                                                 op0=ALU.mult, op1=ALU.mult).then_inc(stats_done, 1)
                    if at == 4:
                        dve.wait_ge(tr_done, n + 1)
                        dve.tensor_copy(hT[:, 0, cols], psP[:, 0, :]).then_inc(hT_done, 1)
                    if at == 6:
                        rows = slice(EI_ROWS[1], P)
                        dve.wait_ge(ei_hi_done, n + 1)
                        if not (first and t == 0):
                            dve.wait_ge(ei_lo_done, n)
                        dve.tensor_tensor(ei_f[rows, :], psP[rows, 0, :], eip_n[rows, cols], ALU.subtract)\
                           .then_inc(ei_rest_done, 1)
                    if at == 8:
                        rows = slice(EI_ROWS[2], P)
                        dve.wait_ge(ei_mid_done, b * T + t + 1)
                        dve.tensor_tensor(eip_n[rows, cols], ei_f[rows, :], eip_n[rows, cols], ALU.subtract)\
                            .then_inc(ei_lo_done, 1)
                n = s - WH_W - 1
                if 0 <= n < BLK and n % 2 == 1:
                    dve.wait_ge(wh_proj, b * BLK + n + 1)
                    if n == 1 and not first:
                        dve.wait_ge(xf_done, b * (2 * H))
                    dve.tensor_copy(wh[:, n].rearrange("p h e -> p (h e)"), psP[:, 1, 0:H * W1])\
                       .then_inc(wh_done[1], 1)
                ei, ej = wh[:, :, :, D], wh[:, :, :, D + 1]
                if s == MAX_W:
                    for i in range(2):
                        dve.wait_ge(wh_done[i], b * (BLK // 2) + BLK // 2)
                    dve.tensor_reduce(mx_p[:, :], ej.rearrange("p k h -> p h k"), AX.X, ALU.max).then_inc(mx_part, 1)
                if s == MAX_W + 2:
                    dve.wait_ge(mx_turned, b + 1)
                    linker(mx_chain, b * 4)(dve.tensor_reduce(mx[:, :], psP[0:H, 0, 0:P], AX.X, ALU.max))
                    dve.tensor_scalar(mx_d[:, :], ident[0:H, 0:H], mx[:, 0:1], None, ALU.mult).then_inc(mx_diag, 1)
                if s == MAX_W + 4:
                    link = linker(mx_chain, b * 4 + 1)
                    dve.wait_ge(mx_done, b + 1)
                    link(dve.tensor_scalar(cen[:, :], psP[:, 1, 0:H], -SHIFT, None, ALU.add))
                    cen_bc = cen[:, None, :].to_broadcast([P, BLK, H])
                    dve.tensor_tensor(xq[:, 0], ej, cen_bc, ALU.subtract)
                    if not first:
                        dve.wait_ge(cq_done, b)
                    dve.tensor_scalar(bigj_n[:, :, :], ej, BIG, None, ALU.mult)
                    link(dve.tensor_tensor(cq_n[:, 1], ei, cen_bc, ALU.add))
                    link(dve.tensor_scalar(cq_n[:, 0], cq_n[:, 1], 0.0, None, ALU.min))
                    dve.tensor_scalar(cq_n[:, 1], cq_n[:, 1], 0.0, None, ALU.max).then_inc(d_done, 1)
                if s == EIP_W:
                    if not first:
                        dve.wait_ge(ei_done, b * U)
                    dve.wait_ge(ei_lo_done, b * T + T)
                    dve.tensor_copy(eip[:, :], eip_n[:, :]).then_inc(eip_done, 1)
                low(b, s, 0) if s in (XY_W[0][3], XY_W[0][3] + 1) else None
                if first and LN_W[0] + 2 <= s < LN_W[0] + 2 + BLK // 2:
                    kb = BLK // 2 + s - LN_W[0] - 2
                    dve.tensor_scalar(adj[:, kb, :], mask[:, kb, :], 0.0, None, ALU.is_gt).then_inc(adj_done, 1)
                if first and s == SLOTS - 1:
                    dve.wait_ge(adj_done, BLK)

            dve.memset(w_ei[:, :, :], 0.0)
            dve.wait_ge(const_in, 64)
            link = linker(w_chain, 0)
            for c in range(FH):
                for part in range(2):
                    link(dve.tensor_tensor(xf[:, 1, 0:H, 0:D], w_all[:, c, :, 0:D],
                                           xf[:, 0, part * H:part * H + H, 0:D], ALU.mult))
                    link(dve.tensor_reduce(w_all[:, c, :, D + part], xf[:, 1, 0:H, 0:D], AX.X, ALU.add))
                for row in EI_ROWS:
                    ins = dve.tensor_copy(w_ei[:, c, row:row + H], w_all[:, c, :, D])
            ins.then_inc(w_done, 1)
            dve.memset(rden[:, 0, :], 1.0).then_inc(piece_free, KCH - 1)
            dve.memset(rden[:, 1, :], 1.0).then_inc(red_done, TB)
            dve.memset(mv[:, :, :], 0.0).then_inc(o_done, 2)
            dve.memset(var[:, :], 0.0).then_inc(acc_done, TB)
            dve.memset(tmp[:, :], 0.0).then_inc(xo_used, 1)
            run(dve, work, prepare)

        @block.tensor
        def _(pe):
            def spread_ei(b, u):
                t, hd = u % T, u // T
                pe.matmul(psE[:, u % 2, :], sel[:, hd, :], eip[:, t * TW:(t + 1) * TW], start=True, stop=True)\
                  .then_inc(ei_done, 1)

            def work(b, s, first, last):
                if s >= SLOTS:
                    return
                u, c = s // KCH, s % KCH
                unit, hd, t = b * U + u, u // T, u % T
                pe.wait_ge(neg_done, unit * KCH + c + 1)
                if t == 0 and c == 0:
                    pe.wait_ge(xy_done, b * (2 * H) + 2 * hd + 2)
                if c == 0 and u + 1 < U:
                    spread_ei(b, u + 1)
                if c == 0 and u + 1 == U and not last:
                    pe.wait_ge(eip_done, b + 2)
                    spread_ei(b, 0)
                for j in range(TB):
                    if c == 0:
                        pe.wait_ge(red_done, unit * TB + j + 1)
                    for k in range(KC):
                        kb = KC * c + k
                        for br, part in enumerate((pos, neg)):
                            ins = pe.matmul(psA[:, j, br * PARTS * XW:(br + 1) * PARTS * XW],
                                            part[:, c, k, j * P:(j + 1) * P],
                                            xy[:, hd % 2, br, kb].rearrange("p c e -> p (c e)"),
                                            start=kb == 0 and br == 0, stop=kb == BLK - 1, skip_group_check=True)
                    if c == KCH - 1:
                        ins.then_inc(acc_done, 1)
                if c < KCH - 1:
                    ins.then_inc(piece_free, 1)

            def prepare(b, s, first):
                for t in range(T):
                    at, cols = s - LN_W[t], slice(t * TW, (t + 1) * TW)
                    if at == 3:
                        pe.wait_ge(h_done, b * T + t + 1)
                        if t:
                            pe.wait_ge(ei_rest_done, b * T + t)
                        for c in range(FH):
                            for j in range(TB):
                                ins = pe.transpose(psP[:, c, j * P:(j + 1) * P],
                                                   xin[:, t % 2, j, c * P:(c + 1) * P], ident[:, :])
                        ins.then_inc(tr_done, 1)
                    if at == 5:
                        pe.wait_ge(hT_done, b * (2 * T) + 2 * t + 2)
                        for c in range(FH):
                            ins = pe.matmul(psP[:, 0, :], w_ei[:, c, :], hT[:, c, cols], start=c == 0, stop=c == FH - 1)
                        ins.then_inc(eiT_done, 1)
                n = s - WH_W
                if 0 <= n < BLK:
                    if n == 0:
                        pe.wait_ge(ei_rest_done, b * T + T)
                    elif n >= 2:
                        pe.wait_ge(wh_done[n % 2], b * (BLK // 2) + n // 2)
                    for c in range(FH):
                        ins = pe.matmul(psP[:, n % 2, 0:H * W1], hT[:, c, n * P:(n + 1) * P],
                                        w_all[:, c].rearrange("p h e -> p (h e)"), start=c == 0, stop=c == FH - 1)
                    ins.then_inc(wh_proj, 1)
                if s == MAX_W + 1:
                    pe.wait_ge(mx_part, b + 1)
                    pe.transpose(psP[0:H, 0, 0:P], mx_p[:, :], ident[:, :]).then_inc(mx_turned, 1)
                if s == MAX_W + 3:
                    pe.wait_ge(mx_diag, b + 1)
                    pe.matmul(psP[:, 1, 0:H], ones[:, :], mx_d[:, :], start=True, stop=True).then_inc(mx_done, 1)
                if first and s == SLOTS - 1:
                    pe.wait_ge(eip_done, 1)
                    spread_ei(0, 0)

            pe.wait_ge(w_done, 1)
            pe.wait_ge(ident_done, 2)
            pe.wait_ge(sel_done, 1)
            run(pe, work, prepare, lag=2)


def build(nc, x, adjT, wqT, wkT, wvT, woT, bq, bk, bv, bo, gamma, beta, w, a1, a2, out):
    x1 = nc.dram_tensor("x_between", [NB, N, F], F32).ap()
    with nc.sbuf_tensor("mask", [P, BLK, N], I8) as mask:
        layer0(nc, mask, x, adjT, wqT, wkT, wvT, woT, bq, bk, bv, bo, gamma, beta, x1, NB)
        layer1(nc, mask, x1, w, a1, a2, out, NB)


def kernel(**inputs):
    import numpy as np
    import concourse.bacc as bacc
    from concourse.bass_utils import run_bass_kernel_spmd

    given = {k: np.asarray(v) for k, v in inputs.items()}
    L0 = {k[7:]: v for k, v in given.items() if k.startswith("L0_gnn_")}
    W, a = given["L1_gnn_W"], given["L1_gnn_a"]
    laid_out = {
        "x": given["x"], "adjT": given["adj"].T,
        "wqT": L0["Wq"].T, "wkT": L0["Wk"].T, "wvT": L0["Wv"].T, "woT": L0["Wo"].T,
        "bq": L0["bq"].reshape(PAIRS, P).T, "bk": L0["bk"].reshape(PAIRS, P).T,
        "bv": L0["bv"], "bo": L0["bo"], "gamma": L0["gamma"], "beta": L0["beta"],
        "w": W.transpose(1, 0, 2), "a1": a[:, :D], "a2": a[:, D:],
    }
    nc = bacc.Bacc("TRN2", target_bir_lowering=False, num_devices=1, dynamic_dma_scratch_size=1024)
    arrays, args = {}, []
    for name, v in laid_out.items():
        arrays[name] = np.ascontiguousarray(v)
        args.append(nc.dram_tensor(name, v.shape, mybir.dt.from_np(v.dtype), kind="ExternalInput").ap())
    args.append(nc.dram_tensor("out", (NB, N, F), F32, kind="ExternalOutput").ap())
    build(nc, *args)
    r = run_bass_kernel_spmd(nc, [arrays], core_ids=[0])
    return r.results[0]["out"]
```

```python
from contextlib import ExitStack

import concourse.bass as bass
from concourse import mybir

ALU = mybir.AluOpType
ACT = mybir.ActivationFunctionType
AX = mybir.AxisListType
F32 = mybir.dt.float32
F32R = mybir.dt.float32r
BF16 = mybir.dt.bfloat16
I32 = mybir.dt.int32
I8 = mybir.dt.int8

P = 128
F = 256
FH = F // P
N = 2048
NB = 8
H = 4
D = F // H
PAIRS = H // 2
BLK = N // P
TW = 512
T = N // TW
TB = TW // P
CHUNK = 256
KPC = CHUNK // P
CH = N // CHUNK
EPS = 1e-5
CLIP = 10.0
SCALE = D ** -0.5
CLIP_RAW = CLIP / SCALE
MAGIC = 1597463007.0

SPC = PAIRS * KPC
STEPS = CH * SPC
HALF = STEPS // 2
CPH = CH // 2
BSTEPS = T * STEPS
GPH = CPH * PAIRS
NCONST = 10
LAG = 2
ES = 6
NS = GPH + 3
LN = 13
SUMS_AT, INV_AT, SPLIT_AT, PICK_AT, RES_AT = 2, 2, 6, 7, 8
PROJ_AT, LN_AT = 2, 6
QUERY_AT = (6, 9)
EARLY = 2
TAIL = HALF + LN_AT + 7 - EARLY
STATS_AT = (-32, -16, 6, 11)
H_AT = (-27, -11, 11, 16)
TR_AT = (2, 7, 12, 17)
Q_AT = 13
MASK_AT = 5


def ln_moments(dve, link, mv, stats, eps_var, rows, n):
    for j in range(n):
        ins = dve.bn_stats(stats[:, j, :], rows(j))
    link(ins)
    dve.memset(eps_var, 0.0)
    for j in range(n):
        ins = dve.bn_aggr(mv[:, j, :], stats[:, j, :])
    link(ins)


def ln_rsqrt(dve, link, part, y, a, eps_var, mv):
    if part == 0:
        link(dve.tensor_scalar(eps_var, mv[:, :, 1], EPS, None, ALU.add))
        link(dve.tensor_scalar(y.bitcast(I32), eps_var.bitcast(I32), -0.5, MAGIC, ALU.mult, ALU.add))
    else:
        link(dve.scalar_tensor_tensor(out=a, in0=y, scalar=-0.5, in1=y, op0=ALU.mult, op1=ALU.mult))
        link(dve.tensor_tensor(a, a, eps_var, ALU.mult))
        link(dve.scalar_tensor_tensor(out=y, in0=a, scalar=1.5, in1=y, op0=ALU.add, op1=ALU.mult))


def linker(dve, chain, before, part=None):
    count = [0 if part is None else 2 + (2 + 3 * (part - 1) if part else 0)]

    def link(ins):
        count[0] += 1
        ins.then_inc(chain, 1)
        dve.wait_ge(chain, before + count[0])
    return link


def layer0(nc, mask, x, adjT, wqT, wkT, wvT, woT, bq, bk, bv, bo, gamma, beta, x1, nb):
    with ExitStack() as ctx:
        def sb(name, shape, dt=F32):
            return ctx.enter_context(nc.sbuf_tensor(name, shape, dt))

        def ps(name, shape, dt=F32):
            return ctx.enter_context(nc.psum_tensor(name, shape, dt))

        def sem(name):
            return ctx.enter_context(nc.semaphore(name))

        w_s = sb("w_s", [P, 2, 3 * FH, F], F32R)
        w_o = sb("w_o", [P, FH, F])
        b_q, b_k = sb("b_q", [P, PAIRS]), sb("b_k", [P, PAIRS])
        b_v, b_o, g_row, be_row = (sb(n, [P, F]) for n in ("b_v", "b_o", "g_row", "be_row"))
        ident = sb("ident", [P, P])
        hot = sb("hot", [P, CPH, 32])
        lo_rows = sb("lo_rows", [P, 1])
        pick = sb("pick", [P, GPH, P], F32R)
        xin = sb("xin", [P, 2, TB, F])
        qT = sb("qT", [P, PAIRS, N])
        kS = sb("kS", [P, H, N], F32R)
        v_sb = sb("v_sb", [P, BLK, F])
        stats = sb("stats", [P, TB, 6])
        mv = sb("mv", [P, TB, 2])
        var = sb("var", [P, TB])
        rs = sb("rs", [P, BLK])
        nmr = sb("nmr", [P, BLK])
        tmp = sb("tmp", [P, TB])
        qM = sb("qM", [P, 2, 2, H, TW], F32R)
        e_sb = sb("e_sb", [P, ES, 2, TW])
        num = sb("num", [P, NS, TW])
        r_f = sb("r_f", [P, TW])
        r_s = sb("r_s", [P, TW], F32R)
        ctxT = sb("ctxT", [P, PAIRS, TW])
        xr = sb("xr", [P, TB, F])
        hy = sb("hy", [P, TB, F])
        st2 = sb("st2", [P, TB, 6])
        mv2 = sb("mv2", [P, TB, 2])
        rs2 = sb("rs2", [P, TB])
        tmp2 = sb("tmp2", [P, TB])
        var2 = sb("var2", [P, TB])
        credit = sb("credit", [P, 1])

        psS = ps("psS", [P, 2, 2, TW])
        psN = ps("psN", [P, PAIRS, TW])
        psD = ps("psD", [P, TW])
        psM = ps("psM", [P, TW])

        const_in = sem("const_in")
        adj_in = [sem(f"adj_in{i}") for i in range(2)]
        mask_done = [sem(f"mask_done{i}") for i in range(2)]
        ident_done = sem("ident_done")
        consts_done = sem("consts_done")
        pool_chain = sem("pool_chain")
        x_in = [sem(f"x_in{i}") for i in range(2)]
        ln_chain, ln2_chain = sem("ln_chain"), sem("ln2_chain")
        stats_done = sem("stats_done")
        h_done = sem("h_done")
        tr_done = sem("tr_done")
        w_hi_done, w_lo_done = sem("w_hi_done"), sem("w_lo_done")
        hT_hi_done, hT_lo_done = sem("hT_hi_done"), sem("hT_lo_done")
        qT_done = sem("qT_done")
        kproj_done = sem("kproj_done")
        khi_done = sem("khi_done")
        klo_done = sem("klo_done")
        vproj_done = sem("vproj_done")
        v_done = sem("v_done")
        qproj_done = sem("qproj_done")
        qhi_done = sem("qhi_done")
        qlo_once = sem("qlo_once")
        qlo_done = sem("qlo_done")
        scores_done = sem("scores_done")
        clip_done = sem("clip_done")
        exp_done = sem("exp_done")
        num_done = sem("num_done")
        numcopy_done = sem("numcopy_done")
        sums_done = sem("sums_done")
        sums_read = sem("sums_read")
        inv_done = sem("inv_done")
        inv_hi_done = sem("inv_hi_done")
        r_done = sem("r_done")
        bcast_done = sem("bcast_done")
        norm_done = sem("norm_done")
        ctx_done = sem("ctx_done")
        oproj_done = sem("oproj_done")
        xr_in = sem("xr_in")
        hr_done = sem("hr_done")
        hb_done = sem("hb_done")
        y_done = sem("y_done")
        yn_done = sem("yn_done")
        affine_chain = sem("affine_chain")
        o_done = sem("o_done")
        x1_out = sem("x1_out")

        stage = [e_sb[:, 0:4, :, :].rearrange("p s a w -> p (s a) w").bitcast(I32), num[:, 0:8, :].bitcast(I32)]
        w_f = v_sb[:, 0:3 * FH, :]

        def hT(t, part, c=None):
            halves = qM[:, 1, part, FH * (t % 2):FH * (t % 2) + FH, :]
            return halves if c is None else halves[:, c, :]
        adj_v = adjT.rearrange("(k p) n -> p k n", p=P)
        x_v = x.rearrange("b (t j p) f -> b t p j f", p=P, j=TB)
        x1_v = x1.rearrange("b (t j p) f -> b t p j f", p=P, j=TB)
        HALVES = 2 * T
        GROUPS = HALVES * GPH
        SUMS = T * (2 * GPH - PAIRS)

        def sums_until(half, i):
            if half % 2 == 0:
                return half * GPH - half // 2 * PAIRS + max(i, i % PAIRS + PAIRS) + 1 - PAIRS
            return half * GPH - (half + 1) // 2 * PAIRS + i + 1

        def place(s):
            return s % STEPS // SPC * KPC + s % KPC, s // KPC % PAIRS

        def chunk_sums_until(s):
            return s // SPC * KPC + s % KPC + 1

        def later_stage(s):
            half = s // HALF - 1
            tile, st = divmod(s - HALF, STEPS)
            if s >= BSTEPS + HALF - EARLY:
                tile, st = T, s - (BSTEPS + HALF - EARLY)
            return (half if 0 <= half < HALVES else None, s % HALF,
                    tile - 1 if 1 <= tile <= T else None, st)

        def next_query(s):
            t = s // STEPS + 1
            return (t if t < T and s % STEPS < HALF else None), s % STEPS

        def tile_of(v, b, t):
            return v[bass.ds(b, 1), t:t + 1].rearrange("o q p j f -> (o q p) j f")

        block = ctx.enter_context(nc.Block())

        @block.sync
        def _(sp):
            def load_x(b, t, first=False):
                if not (first and t < 2):
                    sp.wait_ge(tr_done, b * T + t - 1)
                sp.dma_start(xin[:, t % 2], tile_of(x_v, b, t)).then_inc(x_in[t % 2], 16)

            def load_adjacency(t):
                for k in range(2):
                    if t >= 1:
                        sp.wait_ge(mask_done[k], t)
                    sp.dma_start(stage[k], adj_v[:, 8 * k:8 * k + 8, t * TW:(t + 1) * TW]).then_inc(adj_in[k], 16)

            def load_residual(b, t):
                sp.wait_ge(x1_out, b * (16 * T) + 16 * t + 16)
                sp.dma_start(xr[:, :, :], tile_of(x_v, b, t)).then_inc(xr_in, 16)

            def store(b, t):
                sp.wait_ge(o_done, b * T + t + 1)
                sp.dma_start(tile_of(x1_v, b, t), hy[:, :, :]).then_inc(x1_out, 16)

            def batch(b, last):
                if not last:
                    load_x(b + 1, 0)
                    load_x(b + 1, 1)
                for t in range(T - 1):
                    load_residual(b, t)
                    store(b, t)
                load_residual(b, T - 1)
                if not last:
                    load_x(b + 1, 2)
                    load_x(b + 1, 3)
                store(b, T - 1)

            load_x(0, 0, True)
            load_x(0, 1, True)
            for dst, src in ((w_f[:, 0:2], wkT), (w_f[:, 2:4], wvT), (w_f[:, 4:6], wqT), (w_o[:, :, :], woT)):
                sp.dma_start(dst, src.rearrange("(c p) n -> p c n", p=P)).then_inc(const_in, 16)
            sp.dma_start(b_q[:, :], bq).then_inc(const_in, 16)
            sp.dma_start(b_k[:, :], bk).then_inc(const_in, 16)
            for dst, src in ((b_v, bv), (b_o, bo), (g_row, gamma), (be_row, beta)):
                sp.dma_start(dst[:, :], src.partition_broadcast(P)).then_inc(const_in, 16)
            load_adjacency(0)
            load_x(0, 2, True)
            load_adjacency(1)
            load_x(0, 3, True)
            load_adjacency(2)
            load_adjacency(3)
            if nb > 1:
                with sp.Fori(0, nb - 1) as b:
                    batch(b, False)
            batch(nb - 1, True)
            sp.wait_ge(x1_out, nb * T * 16 + 16)

        @block.gpsimd
        def _(pool):
            count = [0]

            def chain(ins):
                count[0] += 1
                ins.then_inc(pool_chain, 1)
                pool.wait_ge(pool_chain, count[0])

            pool.memset(credit[:, :], 0.0).then_inc(x1_out, 16)
            chain(pool.memset(ident[:, :], 0.0))
            pool.affine_select(out=ident[:, :], in_=ident[:, :], compare_op=ALU.not_equal, fill=1.0,
                               base=0, pattern=[[-1, P]], channel_multiplier=1).then_inc(ident_done, 1)
            chain(pool.memset(hot[:, :, :], 0.0))
            for c in range(CPH):
                chain(pool.memset(hot[:, c, :].rearrange("p (a r) -> p a r", r=CPH)[:, :, c], 1.0))
            chain(pool.memset(lo_rows[:, :], 0.0))
            for q in range(H):
                for c in range(CPH):
                    chain(pool.affine_select(out=lo_rows[:, :], in_=lo_rows[:, :], compare_op=ALU.not_equal,
                                             fill=-1.0, base=-(32 * q + CPH + c), pattern=[[0, 1]],
                                             channel_multiplier=1))
            pick_f = ctxT[:, 0, 0:P]
            for g in range(GPH):
                c, pair = g // PAIRS, g % PAIRS
                chain(pool.memset(pick_f, 0.0))
                for i in range(2):
                    for part in range(2):
                        row = 32 * (2 * pair + i) + CPH * part + c
                        chain(pool.affine_select(out=pick_f[:, 64 * i:64 * i + 64],
                                                 in_=pick_f[:, 64 * i:64 * i + 64],
                                                 compare_op=ALU.not_equal, fill=1.0, base=-row,
                                                 pattern=[[0, 64]], channel_multiplier=1))
                ins = pool.tensor_copy(pick[:, g, :], pick_f)
                if g < GPH - 1:
                    chain(ins)
            ins.then_inc(consts_done, 1)
            pool.wait_ge(const_in, 16 * NCONST)

            def step(b, s):
                half, ss, t, st = later_stage(s)
                i = ss - PICK_AT - 1
                if half is not None and 0 <= i < GPH:
                    pair, slot = i % PAIRS, (half * GPH + i) % NS
                    if half % 2 == 0 and i < 2 * PAIRS:
                        if i >= PAIRS:
                            pool.wait_ge(norm_done, b * GROUPS + half * GPH + i + 1)
                            if half >= 2:
                                pool.wait_ge(oproj_done, b * (2 * T) + half)
                            pool.tensor_tensor(ctxT[:, pair, :], num[:, (slot - PAIRS) % NS, :], num[:, slot, :],
                                               ALU.add).then_inc(ctx_done, 1)
                    else:
                        pool.wait_ge(norm_done, b * GROUPS + half * GPH + i + 1)
                        before = (half, i - PAIRS) if i >= PAIRS else (half - 1, GPH + i - PAIRS)
                        pool.wait_ge(ctx_done, b * SUMS + sums_until(*before))
                        pool.tensor_tensor(ctxT[:, pair, :], ctxT[:, pair, :], num[:, slot, :], ALU.add)                            .then_inc(ctx_done, 1)
                if half is not None and half % 2 == 1 and ss == RES_AT + 2:
                    pool.wait_ge(hr_done, b * T + half // 2 + 1)
                    pool.tensor_tensor(hy[:, :, :], hy[:, :, :], b_o[:, None, :].to_broadcast([P, TB, F]),
                                       ALU.add).then_inc(hb_done, 1)
                if t is not None and st == LN_AT + 6:
                    pool.wait_ge(yn_done, b * T + t + 1)
                    pool.tensor_tensor(hy[:, :, :], hy[:, :, :], g_row[:, None, :].to_broadcast([P, TB, F]),
                                       ALU.mult).then_inc(affine_chain, 1)
                    pool.wait_ge(affine_chain, b * (2 * T) + 2 * t + 1)
                    pool.wait_ge(xr_in, b * (16 * T) + 16 * t + 16)
                    pool.tensor_tensor(hy[:, :, :], hy[:, :, :], xr[:, :, :], ALU.add).then_inc(affine_chain, 1)
                    pool.wait_ge(affine_chain, b * (2 * T) + 2 * t + 2)
                    pool.tensor_tensor(hy[:, :, :], hy[:, :, :], be_row[:, None, :].to_broadcast([P, TB, F]),
                                       ALU.add).then_inc(o_done, 1)

            with pool.Fori(0, nb) as b:
                for s in range(HALF, BSTEPS + TAIL):
                    step(b, s)

        @block.scalar
        def _(act):
            def q_high(b, t, pair):
                act.wait_ge(qT_done, b * (T * PAIRS) + t * PAIRS + pair + 1)
                for i in range(2):
                    rows = slice(64 * i, 64 * i + 64)
                    for j in range(2):
                        ins = act.activation(qM[64 * j:64 * j + 64, t % 2, 0, 2 * pair + i, :],
                                             qT[rows, pair, t * TW:(t + 1) * TW], ACT.Copy)
                ins.then_inc(qhi_done, 1)

            def q_low_twice(b, t, pair):
                act.wait_ge(qlo_once, b * (T * PAIRS) + t * PAIRS + pair + 1)
                for i in range(2):
                    rows, other = slice(64 * i, 64 * i + 64), slice(64 - 64 * i, 128 - 64 * i)
                    hd = 2 * pair + i
                    ins = act.activation(qM[other, t % 2, 1, hd, :], qM[rows, t % 2, 1, hd, :].bitcast(F32), ACT.Copy)
                ins.then_inc(qlo_done, 1)

            def prepare(b, v):
                for t in range(T):
                    if v == H_AT[t]:
                        act.wait_ge(stats_done, b * T + t + 1)
                        for j in range(TB):
                            n = TB * t + j
                            ins = act.activation(xin[:, t % 2, j, :], xin[:, t % 2, j, :], ACT.Relu,
                                                 bias=nmr[:, n:n + 1], scale=rs[:, n:n + 1])
                        ins.then_inc(h_done, 1)
                    if v == TR_AT[t] + 1:
                        act.wait_ge(tr_done, b * T + t + 1)
                        act.activation(hT(t, 0), psS[:, 0, :, :], ACT.Copy).then_inc(hT_hi_done, 1)
                    pair = v - TR_AT[t] - 2
                    if 0 <= pair < PAIRS:
                        act.wait_ge(kproj_done, b * (T * PAIRS) + t * PAIRS + pair + 1)
                        for i in range(2):
                            rows = slice(64 * i, 64 * i + 64)
                            ins = act.activation(kS[rows, 2 * pair + i, t * TW:(t + 1) * TW],
                                                 psS[rows, 1, pair, :], ACT.Identity,
                                                 bias=b_k[rows, pair:pair + 1])
                        ins.then_inc(khi_done, 1)
                    pair = v - TR_AT[t] - 3
                    if 0 <= pair < PAIRS:
                        act.wait_ge(qproj_done, b * (T * PAIRS) + t * PAIRS + pair + 1)
                        act.activation(qT[:, pair, t * TW:(t + 1) * TW], psS[:, 0, pair, :], ACT.Identity,
                                       bias=b_q[:, pair:pair + 1]).then_inc(qT_done, 1)
                if 0 <= v - Q_AT < PAIRS:
                    q_high(b, 0, v - Q_AT)
                if 0 <= v - Q_AT - 3 < PAIRS:
                    q_low_twice(b, 0, v - Q_AT - 3)

            def step(b, s):
                half, ss, _, _ = later_stage(s)
                if s >= 2 * LAG and s % 2 == 0 and s < BSTEPS + 2 * LAG:
                    g = s // 2 - LAG
                    act.wait_ge(num_done, b * GROUPS + g + 1)
                    if g >= NS:
                        act.wait_ge(ctx_done, b * SUMS + sums_until((g - NS) // GPH, (g - NS) % GPH))
                    act.activation(num[:, g % NS, :], psN[:, g % PAIRS, :], ACT.Copy).then_inc(numcopy_done, 1)
                if half is not None and ss == SUMS_AT:
                    act.wait_ge(sums_done, b * (BSTEPS // 2) + (half + 1) * CPH * KPC)
                    if half >= 1:
                        act.wait_ge(r_done, b * HALVES + half)
                    act.activation(r_f[:, :], psD[:, :], ACT.Copy).then_inc(sums_read, 1)
                if half is not None and ss == SPLIT_AT:
                    act.wait_ge(inv_done, b * HALVES + half + 1)
                    if half >= 1:
                        act.wait_ge(bcast_done, b * GROUPS + half * GPH)
                    act.activation(r_s[:, :], r_f[:, :], ACT.Copy).then_inc(inv_hi_done, 1)
                if s < BSTEPS:
                    act.wait_ge(clip_done, b * BSTEPS + s + 1)
                    act.activation(e_sb[:, s % ES], e_sb[:, s % ES], ACT.Exp, scale=SCALE).then_inc(exp_done, 1)
                if half is not None and half % 2 == 1 and ss == RES_AT:
                    t = half // 2
                    act.wait_ge(xr_in, b * (16 * T) + 16 * t + 16)
                    for j in range(TB):
                        n = TB * t + j
                        ins = act.activation(hy[:, j, :], xr[:, j, :], ACT.Relu, bias=nmr[:, n:n + 1],
                                             scale=rs[:, n:n + 1])
                    ins.then_inc(hr_done, 1)
                t, st = next_query(s)
                if t is not None and st - 1 in QUERY_AT:
                    q_high(b, t, QUERY_AT.index(st - 1))
                if t is not None and st - 4 in QUERY_AT:
                    q_low_twice(b, t, QUERY_AT.index(st - 4))

            for v in range(-STEPS, TAIL):
                if v == TR_AT[0]:
                    act.wait_ge(const_in, 16 * NCONST)
                    act.activation(w_s[:, 0], w_f, ACT.Copy).then_inc(w_hi_done, 1)
                prepare(0, v)
                if v - MASK_AT in TR_AT:
                    t = TR_AT.index(v - MASK_AT)
                    act.wait_ge(adj_in[1], 16 * (t + 1))
                    act.activation(mask[:, 8:16, t * TW:(t + 1) * TW], stage[1], ACT.Copy,
                                   bias=-CLIP_RAW, scale=2 * CLIP_RAW).then_inc(mask_done[1], 1)
            act.wait_ge(mask_done[0], T)
            act.wait_ge(mask_done[1], T)
            if nb > 1:
                with act.Fori(0, nb - 1) as b:
                    for s in range(BSTEPS + TAIL):
                        step(b, s)
                        prepare(b + 1, s - BSTEPS)
            for s in range(BSTEPS + TAIL):
                step(nb - 1, s)

        @block.vector
        def _(dve):
            def q_low(b, t, pair, i):
                if i == 0:
                    dve.wait_ge(qhi_done, b * (T * PAIRS) + t * PAIRS + pair + 1)
                rows = slice(64 * i, 64 * i + 64)
                hd = 2 * pair + i
                ins = dve.scalar_tensor_tensor(
                    out=qM[rows, t % 2, 1, hd, :], in0=qT[rows, pair, t * TW:(t + 1) * TW],
                    scalar=0.0, in1=qM[rows, t % 2, 0, hd, :].bitcast(F32), op0=ALU.add, op1=ALU.subtract)
                if i == 1:
                    ins.then_inc(qlo_once, 1)

            def prepare(b, v, first):
                for t in range(T):
                    blocks = slice(TB * t, TB * t + TB)
                    if v == STATS_AT[t]:
                        dve.wait_ge(x_in[t % 2], b * (8 * T) + 16 * (t // 2) + 16)
                        ln_moments(dve, linker(dve, ln_chain, (b * T + t) * LN), mv, stats, var[:, :],
                                   lambda j: xin[:, t % 2, j, :], TB)
                    part = v - STATS_AT[t] - 1
                    if 0 <= part < 4:
                        if part == 0 and t == T - 1 and not first:
                            dve.wait_ge(hr_done, b * T)
                        ln_rsqrt(dve, linker(dve, ln_chain, (b * T + t) * LN, part), part, rs[:, blocks], tmp[:, :],
                                 var[:, :], mv)
                    if part == 3:
                        dve.scalar_tensor_tensor(out=nmr[:, blocks], in0=mv[:, :, 0], scalar=-1.0, in1=rs[:, blocks],
                                                 op0=ALU.mult, op1=ALU.mult).then_inc(stats_done, 1)
                    if v == TR_AT[t] + 1:
                        dve.wait_ge(hT_hi_done, b * T + t + 1)
                        dve.scalar_tensor_tensor(out=hT(t, 1), in0=psS[:, 0, :, :], scalar=0.0,
                                                 in1=hT(t, 0).bitcast(F32), op0=ALU.add, op1=ALU.subtract)\
                           .then_inc(hT_lo_done, 1)
                    pair = v - TR_AT[t] - 2
                    if 0 <= pair < PAIRS:
                        dve.wait_ge(khi_done, b * (T * PAIRS) + t * PAIRS + pair + 1)
                        for i in range(2):
                            rows = slice(64 * i, 64 * i + 64)
                            other = slice(64 - 64 * i, 128 - 64 * i)
                            cols = slice(t * TW, (t + 1) * TW)
                            ins = dve.scalar_tensor_tensor(
                                out=kS[other, 2 * pair + i, cols], in0=psS[rows, 1, pair, :],
                                scalar=b_k[rows, pair:pair + 1],
                                in1=kS[rows, 2 * pair + i, cols].bitcast(F32),
                                op0=ALU.add, op1=ALU.subtract)
                        ins.then_inc(klo_done, 1)
                    j = v - TR_AT[t] - 4
                    if 0 <= j < TB // 2:
                        n = TB * t + 2 * j
                        dve.wait_ge(vproj_done, b * (BLK // 2) + n // 2 + 1)
                        dve.tensor_tensor(v_sb[:, n:n + 2, :],
                                          psN[:, j, :].rearrange("p (a f) -> p a f", a=2),
                                          b_v[:, None, :].to_broadcast([P, 2, F]), ALU.add).then_inc(v_done, 1)
                pair = v - Q_AT - 1
                if 0 <= pair < PAIRS:
                    for i in range(2):
                        q_low(b, 0, pair, i)

            def step(b, s):
                half, ss, t, st = later_stage(s)
                i = ss - PICK_AT - 1
                if half is not None and 0 <= i < GPH:
                    slot = (half * GPH + i) % NS
                    dve.wait_ge(bcast_done, b * GROUPS + half * GPH + i + 1)
                    dve.wait_ge(numcopy_done, b * GROUPS + half * GPH + i + 1)
                    dve.tensor_tensor(num[:, slot, :], num[:, slot, :], psM[:, :], ALU.mult).then_inc(norm_done, 1)
                if t is not None and st in (PROJ_AT + 1, PROJ_AT + 3):
                    j = (st - PROJ_AT) // 2
                    dve.wait_ge(oproj_done, b * (2 * T) + 2 * t + j + 1)
                    dve.wait_ge(hb_done, b * T + t + 1)
                    dve.tensor_tensor(hy[:, 2 * j:2 * j + 2, :], psM[:, :].rearrange("p (a f) -> p a f", a=2),
                                      hy[:, 2 * j:2 * j + 2, :], ALU.add).then_inc(y_done, 1)
                if s < BSTEPS:
                    kb, _ = place(s)
                    cols = slice(s // STEPS * TW, (s // STEPS + 1) * TW)
                    if s >= ES:
                        dve.wait_ge(sums_done, b * (BSTEPS // 2) + chunk_sums_until(s - ES))
                    dve.wait_ge(scores_done, b * BSTEPS + s + 1)
                    dve.scalar_tensor_tensor(
                        out=e_sb[:, s % ES], in0=psS[:, s % 2], scalar=-CLIP_RAW,
                        in1=mask[:, kb, cols][:, None, :].to_broadcast([P, 2, TW]),
                        op0=ALU.max, op1=ALU.min).then_inc(clip_done, 1)
                if half is not None and INV_AT <= ss < INV_AT + TB:
                    cols = slice((ss - INV_AT) * P, (ss - INV_AT + 1) * P)
                    if ss == INV_AT:
                        dve.wait_ge(sums_read, b * HALVES + half + 1)
                    ins = dve.reciprocal(r_f[:, cols], r_f[:, cols])
                    if ss == INV_AT + TB - 1:
                        ins.then_inc(inv_done, 1)
                if half is not None and ss == SPLIT_AT:
                    dve.wait_ge(inv_hi_done, b * HALVES + half + 1)
                    dve.scalar_tensor_tensor(out=r_s[:, :], in0=r_s[:, :].bitcast(F32), scalar=lo_rows[:, 0:1],
                                             in1=r_f[:, :], op0=ALU.mult, op1=ALU.add).then_inc(r_done, 1)
                if t is not None and LN_AT <= st < LN_AT + 6:
                    n = b * T + t
                    if st == LN_AT:
                        dve.wait_ge(y_done, 2 * n + 2)
                        ln_moments(dve, linker(dve, ln2_chain, n * LN), mv2, st2, var2[:, :], lambda j: hy[:, j, :], TB)
                    elif st < LN_AT + 5:
                        part = st - LN_AT - 1
                        ln_rsqrt(dve, linker(dve, ln2_chain, n * LN, part), part, rs2[:, :], tmp2[:, :], var2[:, :], mv2)
                    else:
                        for j in range(TB):
                            ins = dve.tensor_scalar(hy[:, j, :], hy[:, j, :], mv2[:, j, 0:1], rs2[:, j:j + 1],
                                                    ALU.subtract, ALU.mult)
                        ins.then_inc(yn_done, 1)
                t, st = next_query(s)
                for pair in range(PAIRS):
                    for i in range(2):
                        if t is not None and st == QUERY_AT[pair] + 2 + i:
                            q_low(b, t, pair, i)

            for v in range(-STEPS, TAIL):
                if v == TR_AT[0]:
                    dve.wait_ge(w_hi_done, 1)
                    dve.scalar_tensor_tensor(out=w_s[:, 1], in0=w_f, scalar=0.0, in1=w_s[:, 0].bitcast(F32),
                                             op0=ALU.add, op1=ALU.subtract).then_inc(w_lo_done, 1)
                prepare(0, v, True)
                if v - MASK_AT in TR_AT:
                    t = TR_AT.index(v - MASK_AT)
                    dve.wait_ge(adj_in[0], 16 * (t + 1))
                    dve.tensor_scalar(mask[:, 0:8, t * TW:(t + 1) * TW], stage[0], 2 * CLIP_RAW, -CLIP_RAW,
                                      ALU.mult, ALU.add).then_inc(mask_done[0], 1)
            dve.wait_ge(consts_done, 1)
            dve.wait_ge(mask_done[0], T)
            dve.wait_ge(mask_done[1], T)
            if nb > 1:
                with dve.Fori(0, nb - 1) as b:
                    for s in range(BSTEPS + TAIL):
                        step(b, s)
                        prepare(b + 1, s - BSTEPS, False)
            for s in range(BSTEPS + TAIL):
                step(nb - 1, s)

        @block.tensor
        def _(pe):
            def product(out, left, right):
                terms = [(c, i, j) for c in range(FH) for i in range(2) for j in range(2)]
                for n, (c, i, j) in enumerate(terms):
                    ins = pe.matmul(out, left(i, c), right(j, c), start=n == 0, stop=n == len(terms) - 1)
                return ins

            def prepare(b, v, first):
                for t in range(T):
                    cols = slice(t * TW, (t + 1) * TW)
                    if v == TR_AT[t]:
                        pe.wait_ge(h_done, b * T + t + 1)
                        if t:
                            pe.wait_ge(qT_done, b * (T * PAIRS) + t * PAIRS)
                        elif not first:
                            pe.wait_ge(clip_done, b * BSTEPS)
                        for c in range(FH):
                            for j in range(TB):
                                ins = pe.transpose(psS[:, 0, c, j * P:(j + 1) * P],
                                                   xin[:, t % 2, j, c * P:(c + 1) * P], ident[:, :])
                        ins.then_inc(tr_done, 1)
                    pair = v - TR_AT[t] - 1
                    if 0 <= pair < PAIRS:
                        if pair == 0:
                            pe.wait_ge(hT_lo_done, b * T + t + 1)
                        if t:
                            pe.wait_ge(klo_done, b * (T * PAIRS) + (t - 1) * PAIRS + pair + 1)
                        product(psS[:, 1, pair, :], lambda i, c: w_s[:, i, c, pair * P:(pair + 1) * P],
                                lambda i, c: hT(t, i, c)).then_inc(kproj_done, 1)
                    pair = v - TR_AT[t] - 2
                    if 0 <= pair < PAIRS:
                        product(psS[:, 0, pair, :], lambda i, c: w_s[:, i, 2 * FH + c, pair * P:(pair + 1) * P],
                                lambda i, c: hT(t, i, c)).then_inc(qproj_done, 1)
                    j = v - TR_AT[t] - 3
                    if 0 <= j < TB // 2:
                        n = TB * t + 2 * j
                        if t:
                            pe.wait_ge(v_done, b * (BLK // 2) + n // 2 - 1)
                        elif not first:
                            pe.wait_ge(numcopy_done, b * GROUPS)
                        for a in range(2):
                            nodes = slice((2 * j + a) * P, (2 * j + a + 1) * P)
                            ins = product(psN[:, j, a * F:(a + 1) * F], lambda i, c: hT(t, i, c)[:, nodes],
                                          lambda i, c: w_s[:, i, FH + c, :])
                        ins.then_inc(vproj_done, 1)
                if v == TAIL - 1:
                    pe.wait_ge(qT_done, b * (T * PAIRS) + T * PAIRS)
                    pe.wait_ge(klo_done, b * (T * PAIRS) + T * PAIRS)
                    pe.wait_ge(v_done, b * (BLK // 2) + BLK // 2)

            def step(b, s):
                if s < BSTEPS:
                    t, (kb, pair) = s // STEPS, place(s)
                    if s >= 2:
                        pe.wait_ge(clip_done, b * BSTEPS + s - 1)
                    if s % STEPS in (0, KPC):
                        pe.wait_ge(qlo_done, b * (T * PAIRS) + t * PAIRS + pair + 1)
                    for i in range(2):
                        hd = 2 * pair + i
                        for part in range(2):
                            ins = pe.matmul(psS[:, s % 2, i, :], kS[:, hd, kb * P:(kb + 1) * P],
                                            qM[:, t % 2, part, hd, :], start=part == 0, stop=part == 1)
                    ins.then_inc(scores_done, 1)
                u = s - LAG
                if 0 <= u < BSTEPS:
                    (kb, pair), g = place(u), u // KPC
                    pe.wait_ge(exp_done, b * BSTEPS + u + 1)
                    if u % KPC == 0 and g >= PAIRS:
                        pe.wait_ge(numcopy_done, b * GROUPS + g - 1)
                    for i in range(2):
                        hd = 2 * pair + i
                        ins = pe.matmul(psN[64 * i:64 * i + 64, pair, :], v_sb[:, kb, hd * D:(hd + 1) * D],
                                        e_sb[:, u % ES, i, :], start=u % KPC == 0, stop=u % KPC == KPC - 1,
                                        skip_group_check=True)
                    if u % KPC == KPC - 1:
                        ins.then_inc(num_done, 1)
                    if pair == PAIRS - 1:
                        c = u // SPC % CPH
                        first, last = u % HALF == KPC, u % HALF == HALF - 1
                        if first and u >= HALF:
                            pe.wait_ge(sums_read, b * HALVES + u // HALF)
                        for hd in range(H):
                            slot = (u - KPC * (PAIRS - 1 - hd // 2)) % ES
                            ins = pe.matmul(psD[32 * hd:32 * hd + 32, :], hot[:, c, :],
                                            e_sb[:, slot, hd % 2, :], start=first, stop=last,
                                            skip_group_check=True)
                        ins.then_inc(sums_done, 1)
                half, ss, t, st = later_stage(s)
                i = ss - PICK_AT
                if half is not None and 0 <= i < GPH:
                    n = half * GPH + i
                    if i == 0:
                        pe.wait_ge(r_done, b * HALVES + half + 1)
                    else:
                        pe.wait_ge(norm_done, b * GROUPS + n)
                    pe.matmul(psM[:, :], pick[:, i, :], r_s[:, :], start=True, stop=True).then_inc(bcast_done, 1)
                if t is not None and st in (PROJ_AT, PROJ_AT + 2):
                    j = (st - PROJ_AT) // 2
                    if j == 0:
                        pe.wait_ge(ctx_done, b * SUMS + sums_until(2 * t + 1, GPH - 1))
                    else:
                        pe.wait_ge(y_done, b * (2 * T) + 2 * t + 1)
                    for a in range(2):
                        col = (2 * j + a) * P
                        for pair in range(PAIRS):
                            ins = pe.matmul(psM[:, a * F:(a + 1) * F], ctxT[:, pair, col:col + P],
                                            w_o[:, pair, :], start=pair == 0, stop=pair == PAIRS - 1)
                    ins.then_inc(oproj_done, 1)

            pe.wait_ge(ident_done, 1)
            for v in range(TAIL):
                if v == TR_AT[0] + 1:
                    pe.wait_ge(w_lo_done, 1)
                prepare(0, v, True)
            pe.wait_ge(consts_done, 1)
            if nb > 1:
                with pe.Fori(0, nb - 1) as b:
                    for s in range(BSTEPS + TAIL):
                        step(b, s)
                        prepare(b + 1, s - BSTEPS, False)
            for s in range(BSTEPS + TAIL):
                step(nb - 1, s)


W1 = D + 2
XW = D + 1
PARTS = 3
KC = 4
KCH = BLK // KC
U = H * T
SLOTS = U * KCH
ROT = 2 * KCH
ALPHA = 0.2
BIG = 2.0 ** 60
SHIFT = 60.0
EI_ROWS = (0, 64, 96)
LN_W = (10, 15, 20, 25)
WH_W = 32
MAX_W = WH_W + BLK
EIP_W = 58
XY_W = ((MAX_W + 6, MAX_W + 8, MAX_W + 11, MAX_W + 12), (4, 9, 11, 12), (14, 20, 22, 23), (28, 36, 38, 39))
ELU_W = (SLOTS - 2, SLOTS + 6)
MAX0_W = (SLOTS, SLOTS + 1, SLOTS + 7, SLOTS + 7)
FIN_W = (SLOTS + 1, SLOTS + 2, SLOTS + 7, SLOTS + 7)


def layer1(nc, mask, x1, w, a1, a2, out, nb):
    with ExitStack() as ctx:
        def sb(name, shape, dt=F32):
            return ctx.enter_context(nc.sbuf_tensor(name, shape, dt))

        def ps(name, shape, dt=F32):
            return ctx.enter_context(nc.psum_tensor(name, shape, dt))

        def sem(name):
            return ctx.enter_context(nc.semaphore(name))

        adj = sb("adj", [P, BLK, N], BF16)
        w_all = sb("w_all", [P, FH, H, W1])
        w_ei = sb("w_ei", [P, FH, P])
        sel = sb("sel", [P, H, P], BF16)
        ident = sb("ident1", [P, P])
        ones = sb("ones1", [H, P])
        xin = sb("xin1", [P, 2, TB, F])
        stats = sb("stats1", [P, TB, 6])
        mv = sb("mv1", [P, TB, 2])
        rs = sb("rs1", [P, 2, TB])
        nmr = sb("nmr1", [P, 2, TB])
        var = sb("var1", [P, TB])
        tmp = sb("tmp1", [P, TB])
        hT = sb("hT1", [P, FH, N])
        wh = sb("wh", [P, BLK, H, W1])
        mx_p = sb("mx_p", [P, H])
        mx = sb("mx", [H, 1])
        mx_d = sb("mx_d", [H, H])
        cen = sb("cen", [P, H])
        xq = sb("xq", [P, 2, BLK, H])
        cq, cq_n = sb("cq", [P, 2, BLK, H]), sb("cq_n", [P, 2, BLK, H])
        bigj, bigj_n = sb("bigj", [P, BLK, H]), sb("bigj_n", [P, BLK, H])
        eip, eip_n = sb("eip", [P, N], BF16), sb("eip_n", [P, N], BF16)
        ei_f = sb("ei_f", [P, TW])
        xf = sb("xf", [P, 2, BLK, XW])
        xy = sb("xy", [P, 2, 2, BLK, PARTS, XW], BF16)
        pos, neg = (mask[:, 8 * i:8 * i + 8, :].rearrange("p k n -> p (k n)").bitcast(BF16)
                    .rearrange("p (c k n) -> p c k n", c=KCH, k=KC) for i in range(2))
        red = sb("red", [P, 2, TB, 2, XW])
        rden = sb("rden", [P, 2, TB])
        o_sb = sb("o_sb", [P, BLK, F])
        em = sb("em", [P, 2, TB, F])
        xo = sb("xo", [P, TB, F])

        psP = ps("psP", [P, 2, TW])
        psE = ps("psE", [P, 2, TW])
        psA = ps("psA", [P, TB, TW])

        const_in = sem("const1_in")
        adj_done = sem("adj1_done")
        ident_done = sem("ident1_done")
        sel_f_done = sem("sel_f_done")
        sel_done = sem("sel_done")
        w_chain = sem("w1_chain")
        w_done = sem("w1_done")
        x_in = [sem(f"x1_in{i}") for i in range(2)]
        ln_chain = sem("ln1_chain")
        stats_done = sem("stats1_done")
        h_done = sem("h1_done")
        tr_done = sem("tr1_done")
        hT_done = sem("hT1_done")
        eiT_done = sem("eiT_done")
        ei_hi_done = sem("ei_hi_done")
        ei_rest_done = sem("ei_rest_done")
        ei_mid_done = sem("ei_mid_done")
        ei_lo_done = sem("ei_lo_done")
        eip_done = sem("eip_done")
        wh_proj = sem("wh_proj")
        wh_done = [sem(f"wh_done{i}") for i in range(2)]
        mx_chain = sem("mx_chain")
        mx_part = sem("mx_part")
        mx_turned = sem("mx_turned")
        mx_diag = sem("mx_diag")
        mx_done = sem("mx_done")
        d_done = sem("d_done")
        q_done = sem("q_done")
        cq_done = sem("cq_done")
        bigj_done = sem("bigj_done")
        xf_done = sem("xf_done")
        hi_done = sem("hi1_done")
        rest_done = sem("rest_done")
        mid_done = sem("mid_done")
        xy_done = sem("xy_done")
        ei_done = sem("ei_done")
        step_done = sem("step_done")
        pos_done = sem("pos_done")
        neg_done = sem("neg_done")
        piece_free = sem("piece_free")
        acc_done = sem("acc_done")
        red_done = sem("red_done")
        mix_chain = sem("mix_chain")
        mix_done = sem("mix_done")
        rden_done = sem("rden_done")
        o_done = sem("o1_done")
        xo_in = sem("xo_in")
        minus_done = sem("minus_done")
        en_done = sem("en_done")
        elu_done = sem("elu_done")
        fin_done = sem("fin_done")
        out_done = [sem(f"out_done{t}") for t in range(T)]

        x_v = x1.rearrange("b (t j p) f -> b t p j f", p=P, j=TB)
        out_v = out.rearrange("b (t j p) f -> b t p j f", p=P, j=TB)

        def tile_of(v, b, t):
            return v[bass.ds(b, 1), t:t + 1].rearrange("o q p j f -> (o q p) j f")

        def run(engine, work, prepare, lag=0):
            for s in range(SLOTS):
                prepare(0, s, True)
            for s in range(ROT):
                work(0, s, first=True, last=nb == 1)
            if nb > 1:
                with engine.Fori(0, nb - 1) as b:
                    for s in range(ROT, SLOTS):
                        work(b, s, first=False, last=False)
                        prepare(b + 1, s + lag, False)
                    for s in range(ROT):
                        work(b + 1, s, first=False, last=False)
            for s in range(ROT, SLOTS + ROT):
                work(nb - 1, s, first=False, last=True)

        def ended_unit(b, s, first):
            u = s // KCH
            if u == 0:
                return None if first else (b - 1, U - 1)
            return (b, u - 1) if u <= U else None

        def output_at(b, s, first, at):
            if s == at:
                return b
            return b - 1 if s + SLOTS == at and not first else None

        block = ctx.enter_context(nc.Block())

        @block.sync
        def _(sp):
            def load_x(b, t, first):
                if not (first and t < 2):
                    sp.wait_ge(tr_done, b * T + t - 1)
                sp.dma_start(xin[:, t % 2], tile_of(x_v, b, t)).then_inc(x_in[t % 2], 16)

            def load_xo(b, t):
                sp.wait_ge(fin_done, b * T + t + 1)
                sp.dma_start(xo[:, :, :], tile_of(x_v, b, t)).then_inc(xo_in, 16)

            def batch(b, last):
                if not last:
                    for t in range(T):
                        load_x(b + 1, t, False)
                for t in range(T):
                    load_xo(b, t)
                    sp.wait_ge(fin_done, b * T + t + 2)
                    sp.dma_start(tile_of(out_v, b, t), o_sb[:, TB * t:TB * t + TB, :]).then_inc(out_done[t], 16)

            load_x(0, 0, True)
            for c in range(FH):
                sp.dma_start(w_all[:, c, :, 0:D], w[c * P:(c + 1) * P, :, :]).then_inc(const_in, 16)
            sp.dma_start(xf[:, 0, 0:H, 0:D], a1.partition_broadcast(P)).then_inc(const_in, 16)
            sp.dma_start(xf[:, 0, H:2 * H, 0:D], a2.partition_broadcast(P)).then_inc(const_in, 16)
            for t in range(1, T):
                load_x(0, t, True)
            if nb > 1:
                with sp.Fori(0, nb - 1) as b:
                    batch(b, False)
            batch(nb - 1, True)
            for t in range(T):
                sp.wait_ge(out_done[t], nb * 16 + 16)

        @block.gpsimd
        def _(pool):
            def mix(b, u):
                unit, hd, t = b * U + u, u // T, u % T
                r, blocks = red[:, u % 2], slice(TB * t, TB * t + TB)
                pool.wait_ge(red_done, unit * TB + 2 * TB)
                if u == 0:
                    pool.wait_ge(cq_done, b + 1)
                for br in range(2):
                    ins = pool.tensor_tensor(r[:, :, br, :], r[:, :, br, :],
                                             cq[:, br, blocks, hd][:, :, None].to_broadcast([P, TB, XW]), ALU.mult)
                ins.then_inc(mix_chain, 1)
                pool.wait_ge(mix_chain, unit + 1)
                pool.tensor_tensor(r[:, :, 0, :], r[:, :, 0, :], r[:, :, 1, :], ALU.add).then_inc(mix_done, 1)
                pool.wait_ge(rden_done, unit + 1)
                if hd == 0:
                    pool.wait_ge(out_done[t], b * 16 + 16)
                pool.tensor_tensor(o_sb[:, blocks, hd * D:(hd + 1) * D], r[:, :, 0, 0:D],
                                   rden[:, u % 2, :][:, :, None].to_broadcast([P, TB, D]), ALU.mult).then_inc(o_done, 1)

            def work(b, s, first, last):
                ended = ended_unit(b, s, first)
                if ended and s % KCH == KCH - 1:
                    mix(*ended)
                for t in range(T):
                    now = output_at(b, s, first, FIN_W[t])
                    if now is not None:
                        rows = slice(TB * t, TB * t + TB)
                        pool.wait_ge(elu_done, now * T + t + 1)
                        pool.wait_ge(xo_in, now * (16 * T) + 16 * t + 16)
                        pool.tensor_tensor(o_sb[:, rows, :], em[:, t % 2], xo[:, :, :], ALU.add).then_inc(fin_done, 1)
                for hd in range(1, H):
                    weigh(b, s, hd, False)

            def weigh(b, s, hd, first):
                mult_at, split_at, _, _ = XY_W[hd]
                for br in range(2):
                    n = b * (2 * H) + 2 * hd + br
                    f, hi = xf[:, br], xy[:, hd % 2, br, :, 0, :]
                    if s == mult_at + br:
                        if hd == 0 and br == 0:
                            pool.wait_ge(q_done, b + 1)
                        if not (first and hd == 0):
                            pool.wait_ge(xy_done, n - 1)
                        pool.tensor_tensor(f[:, :, 0:D], wh[:, :, hd, 0:D],
                                           xq[:, br, :, hd][:, :, None].to_broadcast([P, BLK, D]), ALU.mult)
                        pool.tensor_copy(f[:, :, D:XW], xq[:, br, :, hd][:, :, None]).then_inc(xf_done, 1)
                    if s == split_at + br:
                        pool.wait_ge(hi_done, n + 1)
                        pool.tensor_tensor(f, f, hi, ALU.subtract).then_inc(rest_done, 1)

            def prepare(b, s, first):
                weigh(b, s, 0, first)

            pool.memset(ones[:, :], 1.0).then_inc(out_done[0], 16)
            for t in range(1, T):
                pool.memset(xo[:, t, 0:1], 0.0).then_inc(out_done[t], 16)
            pool.memset(ident[:, :], 0.0).then_inc(ident_done, 1)
            pool.wait_ge(ident_done, 1)
            pool.affine_select(out=ident[:, :], in_=ident[:, :], compare_op=ALU.not_equal, fill=1.0,
                               base=0, pattern=[[-1, P]], channel_multiplier=1).then_inc(ident_done, 1)
            sel_f = em[:, 0, 0:2, :].rearrange("p a f -> p (a f)")
            pool.memset(sel_f, 0.0).then_inc(sel_f_done, 1)
            n = 1
            for hd in range(H):
                for row in EI_ROWS:
                    pool.wait_ge(sel_f_done, n)
                    cols = sel_f[:, hd * P:(hd + 1) * P]
                    pool.affine_select(out=cols, in_=cols, compare_op=ALU.not_equal, fill=1.0, base=-(row + hd),
                                       pattern=[[0, P]], channel_multiplier=1).then_inc(sel_f_done, 1)
                    n += 1
            run(pool, work, prepare)

        @block.scalar
        def _(act):
            def steps(b, u, c):
                unit, hd = b * U + u, u // T
                if c == 0:
                    act.wait_ge(ei_done, unit + 1)
                if c < KCH - 1:
                    act.wait_ge(piece_free, unit * (KCH - 1) + c + 1)
                else:
                    act.wait_ge(acc_done, unit * TB + TB)
                for k in range(KC):
                    kb = KC * c + k
                    ins = act.activation(pos[:, c, k, :], psE[:, u % 2, :], ACT.Sigmoid,
                                         bias=bigj[:, kb, hd:hd + 1], scale=BIG)
                ins.then_inc(step_done, 1)

            def elu(b, tiles):
                for t in tiles:
                    act.wait_ge(o_done, b * U + (U - T + t) + 3)
                    if t >= 2:
                        act.wait_ge(fin_done, b * T + t)
                    act.activation(em[:, t % 2], o_sb[:, TB * t:TB * t + TB, :], ACT.Relu, scale=-1.0)\
                       .then_inc(minus_done, 1)
                for t in tiles:
                    act.wait_ge(minus_done, b * T + t + 1)
                    act.activation(em[:, t % 2], em[:, t % 2], ACT.Exp, scale=-1.0).then_inc(en_done, 1)

            def work(b, s, first, last):
                if s < SLOTS:
                    if s == 0:
                        if not first:
                            act.wait_ge(step_done, b * SLOTS)
                        act.activation(bigj[:, :, :], bigj_n[:, :, :], ACT.Copy).then_inc(bigj_done, 1)
                        act.wait_ge(bigj_done, b + 1)
                    steps(b, s // KCH, s % KCH)
                for i in range(2):
                    now = output_at(b, s, first, ELU_W[i])
                    if now is not None:
                        elu(now, (2 * i, 2 * i + 1))
                for hd in range(1, H):
                    split(b, s, hd, False)

            def split(b, s, hd, first):
                _, hi_at, mid_at, _ = XY_W[hd]
                for br in range(2):
                    n = b * (2 * H) + 2 * hd + br
                    if s == hi_at + br:
                        act.wait_ge(xf_done, n + 1)
                        if not (first and hd == 0):
                            act.wait_ge(acc_done, b * (U * TB) + (hd - 1) * T * TB + TB)
                        act.activation(xy[:, hd % 2, br, :, 0, :], xf[:, br], ACT.Copy).then_inc(hi_done, 1)
                    if s == mid_at + br:
                        act.wait_ge(rest_done, n + 1)
                        act.activation(xy[:, hd % 2, br, :, 1, :], xf[:, br], ACT.Copy).then_inc(mid_done, 1)

            def prepare(b, s, first):
                for t in range(T):
                    at, cols = s - LN_W[t], slice(t * TW, (t + 1) * TW)
                    if at == 3:
                        act.wait_ge(stats_done, b * T + t + 1)
                        for j in range(TB):
                            ins = act.activation(xin[:, t % 2, j, :], xin[:, t % 2, j, :], ACT.Relu,
                                                 bias=nmr[:, t % 2, j:j + 1], scale=rs[:, t % 2, j:j + 1])
                        ins.then_inc(h_done, 1)
                    if at == 5:
                        act.wait_ge(tr_done, b * T + t + 1)
                        act.activation(hT[:, :, cols], psP[:, :, :], ACT.Copy).then_inc(hT_done, 1)
                    if at == 7:
                        act.wait_ge(eiT_done, b * T + t + 1)
                        if t == 0 and not first:
                            act.wait_ge(eip_done, b)
                        act.activation(eip_n[:, cols], psP[:, 0, :], ACT.Copy).then_inc(ei_hi_done, 1)
                    if at == 8:
                        rows = slice(EI_ROWS[1], P)
                        act.wait_ge(ei_rest_done, b * T + t + 1)
                        act.activation(eip_n[rows, cols], ei_f[rows, :], ACT.Copy).then_inc(ei_mid_done, 1)
                n = s - WH_W - 1
                if 0 <= n < BLK and n % 2 == 0:
                    act.wait_ge(wh_proj, b * BLK + n + 1)
                    if n == 0 and not first:
                        act.wait_ge(xf_done, b * (2 * H))
                    act.activation(wh[:, n].rearrange("p h e -> p (h e)"), psP[:, 0, 0:H * W1], ACT.Copy)\
                       .then_inc(wh_done[0], 1)
                if s == MAX_W + 5:
                    act.wait_ge(d_done, b + 1)
                    act.activation(xq[:, 1], xq[:, 0], ACT.Exp, scale=ALPHA)
                    act.activation(xq[:, 0], xq[:, 0], ACT.Exp)
                    act.activation(cq_n[:, 0], cq_n[:, 0], ACT.Exp, scale=1.0 - ALPHA)
                    act.activation(cq_n[:, 1], cq_n[:, 1], ACT.Exp, scale=ALPHA - 1.0).then_inc(q_done, 1)
                split(b, s, 0, first)
                if first and LN_W[0] + 2 <= s < LN_W[0] + 2 + BLK // 2:
                    kb = s - LN_W[0] - 2
                    act.activation(adj[:, kb, :], mask[:, kb, :], ACT.Copy, bias=0.5, scale=0.5 / CLIP_RAW)\
                       .then_inc(adj_done, 1)
                if first and s == SLOTS - 1:
                    act.wait_ge(adj_done, BLK)

            act.wait_ge(sel_f_done, 1 + H * PARTS)
            act.activation(sel[:, :, :].rearrange("p h m -> p (h m)"), em[:, 0, 0:2, :].rearrange("p a f -> p (a f)"),
                           ACT.Copy).then_inc(sel_done, 1)
            run(act, work, prepare)

        @block.vector
        def _(dve):
            def piece(b, u, c):
                n = (b * U + u) * KCH + c
                edges = adj[:, KC * c:KC * c + KC, u % T * TW:(u % T + 1) * TW]
                dve.wait_ge(step_done, n + 1)
                dve.tensor_tensor(pos[:, c], pos[:, c], edges, ALU.mult).then_inc(pos_done, 1)
                dve.wait_ge(pos_done, n + 1)
                dve.tensor_tensor(neg[:, c], edges, pos[:, c], ALU.subtract).then_inc(neg_done, 1)

            def reduce(b, u):
                unit = b * U + u
                dve.wait_ge(o_done, unit + 1)
                for j in range(TB):
                    dve.wait_ge(acc_done, unit * TB + TB + j + 1)
                    dve.tensor_reduce(red[:, u % 2, j], psA[:, j, 0:2 * PARTS * XW].rearrange(
                        "p (r c e) -> p r e c", r=2, c=PARTS), AX.X, ALU.add).then_inc(red_done, 1)

            def invert(b, u):
                dve.wait_ge(mix_done, b * U + u + 1)
                dve.reciprocal(rden[:, u % 2, :], red[:, u % 2, :, 0, D]).then_inc(rden_done, 1)

            def work(b, s, first, last):
                u, c = s // KCH, s % KCH
                ended = ended_unit(b, s, first)
                if ended and c == 2:
                    reduce(*ended)
                if s < SLOTS:
                    piece(b, u, c)
                if ended and c == KCH - 1:
                    invert(*ended)
                for t in range(T):
                    now = output_at(b, s, first, MAX0_W[t])
                    if now is not None:
                        dve.wait_ge(en_done, now * T + t + 1)
                        dve.scalar_tensor_tensor(out=em[:, t % 2], in0=em[:, t % 2], scalar=-1.0,
                                                 in1=o_sb[:, TB * t:TB * t + TB, :], op0=ALU.add, op1=ALU.max)\
                           .then_inc(elu_done, 1)
                if s == 4:
                    if not first:
                        dve.wait_ge(mix_chain, b * U)
                    dve.wait_ge(q_done, b + 1)
                    dve.tensor_copy(cq[:, :, :, :], cq_n[:, :, :, :]).then_inc(cq_done, 1)
                for hd in range(1, H):
                    low(b, s, hd)

            def low(b, s, hd):
                for br in range(2):
                    if s == XY_W[hd][3] + br:
                        dve.wait_ge(mid_done, b * (2 * H) + 2 * hd + br + 1)
                        mid, lo = (xy[:, hd % 2, br, :, i, :] for i in (1, 2))
                        dve.tensor_tensor(lo, xf[:, br], mid, ALU.subtract).then_inc(xy_done, 1)

            def prepare(b, s, first):
                for t in range(T):
                    at, cols = s - LN_W[t], slice(t * TW, (t + 1) * TW)
                    n = b * T + t
                    if at == 0:
                        dve.wait_ge(x_in[t % 2], b * (8 * T) + 16 * (t // 2) + 16)
                        ln_moments(dve, linker(dve, ln_chain, n * LN), mv, stats, var[:, :],
                                   lambda j: xin[:, t % 2, j, :], TB)
                    if at in (1, 2):
                        for part in (2 * at - 2, 2 * at - 1):
                            ln_rsqrt(dve, linker(dve, ln_chain, n * LN, part), part, rs[:, t % 2], tmp[:, :],
                                     var[:, :], mv)
                    if at == 2:
                        dve.scalar_tensor_tensor(out=nmr[:, t % 2], in0=mv[:, :, 0], scalar=-1.0, in1=rs[:, t % 2],
                                                 op0=ALU.mult, op1=ALU.mult).then_inc(stats_done, 1)
                    if at == 7:
                        rows = slice(EI_ROWS[1], P)
                        dve.wait_ge(ei_hi_done, n + 1)
                        if not (first and t == 0):
                            dve.wait_ge(ei_lo_done, n)
                        dve.tensor_tensor(ei_f[rows, :], psP[rows, 0, :], eip_n[rows, cols], ALU.subtract)\
                           .then_inc(ei_rest_done, 1)
                    if at == 9:
                        rows = slice(EI_ROWS[2], P)
                        dve.wait_ge(ei_mid_done, b * T + t + 1)
                        dve.tensor_tensor(eip_n[rows, cols], ei_f[rows, :], eip_n[rows, cols], ALU.subtract)\
                            .then_inc(ei_lo_done, 1)
                n = s - WH_W - 1
                if 0 <= n < BLK and n % 2 == 1:
                    dve.wait_ge(wh_proj, b * BLK + n + 1)
                    if n == 1 and not first:
                        dve.wait_ge(xf_done, b * (2 * H))
                    dve.tensor_copy(wh[:, n].rearrange("p h e -> p (h e)"), psP[:, 1, 0:H * W1])\
                       .then_inc(wh_done[1], 1)
                ei, ej = wh[:, :, :, D], wh[:, :, :, D + 1]
                if s == MAX_W:
                    for i in range(2):
                        dve.wait_ge(wh_done[i], b * (BLK // 2) + BLK // 2)
                    dve.tensor_reduce(mx_p[:, :], ej.rearrange("p k h -> p h k"), AX.X, ALU.max).then_inc(mx_part, 1)
                if s == MAX_W + 2:
                    dve.wait_ge(mx_turned, b + 1)
                    linker(dve, mx_chain, b * 4)(dve.tensor_reduce(mx[:, :], psP[0:H, 0, 0:P], AX.X, ALU.max))
                    dve.tensor_scalar(mx_d[:, :], ident[0:H, 0:H], mx[:, 0:1], None, ALU.mult).then_inc(mx_diag, 1)
                if s == MAX_W + 4:
                    link = linker(dve, mx_chain, b * 4 + 1)
                    dve.wait_ge(mx_done, b + 1)
                    link(dve.tensor_scalar(cen[:, :], psP[:, 1, 0:H], -SHIFT, None, ALU.add))
                    cen_bc = cen[:, None, :].to_broadcast([P, BLK, H])
                    dve.tensor_tensor(xq[:, 0], ej, cen_bc, ALU.subtract)
                    if not first:
                        dve.wait_ge(cq_done, b)
                    dve.tensor_scalar(bigj_n[:, :, :], ej, BIG, None, ALU.mult)
                    link(dve.tensor_tensor(cq_n[:, 1], ei, cen_bc, ALU.add))
                    link(dve.tensor_scalar(cq_n[:, 0], cq_n[:, 1], 0.0, None, ALU.min))
                    dve.tensor_scalar(cq_n[:, 1], cq_n[:, 1], 0.0, None, ALU.max).then_inc(d_done, 1)
                if s == EIP_W:
                    if not first:
                        dve.wait_ge(ei_done, b * U)
                    dve.wait_ge(ei_lo_done, b * T + T)
                    dve.tensor_copy(eip[:, :], eip_n[:, :]).then_inc(eip_done, 1)
                low(b, s, 0) if s in (XY_W[0][3], XY_W[0][3] + 1) else None
                if first and LN_W[0] + 2 <= s < LN_W[0] + 2 + BLK // 2:
                    kb = BLK // 2 + s - LN_W[0] - 2
                    dve.tensor_scalar(adj[:, kb, :], mask[:, kb, :], 0.0, None, ALU.is_gt).then_inc(adj_done, 1)
                if first and s == SLOTS - 1:
                    dve.wait_ge(adj_done, BLK)

            dve.memset(w_ei[:, :, :], 0.0)
            dve.wait_ge(const_in, 64)
            link = linker(dve, w_chain, 0)
            for c in range(FH):
                for part in range(2):
                    link(dve.tensor_tensor(xf[:, 1, 0:H, 0:D], w_all[:, c, :, 0:D],
                                           xf[:, 0, part * H:part * H + H, 0:D], ALU.mult))
                    link(dve.tensor_reduce(w_all[:, c, :, D + part], xf[:, 1, 0:H, 0:D], AX.X, ALU.add))
                for row in EI_ROWS:
                    ins = dve.tensor_copy(w_ei[:, c, row:row + H], w_all[:, c, :, D])
            ins.then_inc(w_done, 1)
            dve.memset(rden[:, 0, :], 1.0).then_inc(piece_free, KCH - 1)
            dve.memset(rden[:, 1, :], 1.0).then_inc(red_done, TB)
            dve.memset(mv[:, :, :], 0.0).then_inc(o_done, 2)
            dve.memset(var[:, :], 0.0).then_inc(acc_done, TB)
            dve.memset(tmp[:, :], 0.0).then_inc(fin_done, 1)
            run(dve, work, prepare)

        @block.tensor
        def _(pe):
            def spread_ei(b, u):
                t, hd = u % T, u // T
                pe.matmul(psE[:, u % 2, :], sel[:, hd, :], eip[:, t * TW:(t + 1) * TW], start=True, stop=True)\
                  .then_inc(ei_done, 1)

            def work(b, s, first, last):
                if s >= SLOTS:
                    return
                u, c = s // KCH, s % KCH
                unit, hd, t = b * U + u, u // T, u % T
                pe.wait_ge(neg_done, unit * KCH + c + 1)
                if t == 0 and c == 0:
                    pe.wait_ge(xy_done, b * (2 * H) + 2 * hd + 2)
                if c == 0 and u + 1 < U:
                    spread_ei(b, u + 1)
                if c == 0 and u + 1 == U and not last:
                    pe.wait_ge(eip_done, b + 2)
                    spread_ei(b, 0)
                for j in range(TB):
                    if c == 0:
                        pe.wait_ge(red_done, unit * TB + j + 1)
                    for k in range(KC):
                        kb = KC * c + k
                        for br, part in enumerate((pos, neg)):
                            ins = pe.matmul(psA[:, j, br * PARTS * XW:(br + 1) * PARTS * XW],
                                            part[:, c, k, j * P:(j + 1) * P],
                                            xy[:, hd % 2, br, kb].rearrange("p c e -> p (c e)"),
                                            start=kb == 0 and br == 0, stop=kb == BLK - 1, skip_group_check=True)
                    if c == KCH - 1:
                        ins.then_inc(acc_done, 1)
                if c < KCH - 1:
                    ins.then_inc(piece_free, 1)

            def prepare(b, s, first):
                for t in range(T):
                    at, cols = s - LN_W[t], slice(t * TW, (t + 1) * TW)
                    if at == 4:
                        pe.wait_ge(h_done, b * T + t + 1)
                        if t:
                            pe.wait_ge(ei_rest_done, b * T + t)
                        for c in range(FH):
                            for j in range(TB):
                                ins = pe.transpose(psP[:, c, j * P:(j + 1) * P],
                                                   xin[:, t % 2, j, c * P:(c + 1) * P], ident[:, :])
                        ins.then_inc(tr_done, 1)
                    if at == 6:
                        pe.wait_ge(hT_done, b * T + t + 1)
                        for c in range(FH):
                            ins = pe.matmul(psP[:, 0, :], w_ei[:, c, :], hT[:, c, cols], start=c == 0, stop=c == FH - 1)
                        ins.then_inc(eiT_done, 1)
                n = s - WH_W
                if 0 <= n < BLK:
                    if n == 0:
                        pe.wait_ge(ei_rest_done, b * T + T)
                    elif n >= 2:
                        pe.wait_ge(wh_done[n % 2], b * (BLK // 2) + n // 2)
                    for c in range(FH):
                        ins = pe.matmul(psP[:, n % 2, 0:H * W1], hT[:, c, n * P:(n + 1) * P],
                                        w_all[:, c].rearrange("p h e -> p (h e)"), start=c == 0, stop=c == FH - 1)
                    ins.then_inc(wh_proj, 1)
                if s == MAX_W + 1:
                    pe.wait_ge(mx_part, b + 1)
                    pe.transpose(psP[0:H, 0, 0:P], mx_p[:, :], ident[:, :]).then_inc(mx_turned, 1)
                if s == MAX_W + 3:
                    pe.wait_ge(mx_diag, b + 1)
                    pe.matmul(psP[:, 1, 0:H], ones[:, :], mx_d[:, :], start=True, stop=True).then_inc(mx_done, 1)
                if first and s == SLOTS - 1:
                    pe.wait_ge(eip_done, 1)
                    spread_ei(0, 0)

            pe.wait_ge(w_done, 1)
            pe.wait_ge(ident_done, 2)
            pe.wait_ge(sel_done, 1)
            run(pe, work, prepare, lag=2)


def build(nc, x, adjT, wqT, wkT, wvT, woT, bq, bk, bv, bo, gamma, beta, w, a1, a2, out):
    x1 = nc.dram_tensor("x_between", [NB, N, F], F32).ap()
    with nc.sbuf_tensor("mask", [P, BLK, N], I8) as mask:
        layer0(nc, mask, x, adjT, wqT, wkT, wvT, woT, bq, bk, bv, bo, gamma, beta, x1, NB)
        layer1(nc, mask, x1, w, a1, a2, out, NB)


def kernel(**inputs):
    import numpy as np
    import concourse.bacc as bacc
    from concourse.bass_utils import run_bass_kernel_spmd

    given = {k: np.asarray(v) for k, v in inputs.items()}
    L0 = {k[7:]: v for k, v in given.items() if k.startswith("L0_gnn_")}
    W, a = given["L1_gnn_W"], given["L1_gnn_a"]
    laid_out = {
        "x": given["x"], "adjT": given["adj"].T,
        "wqT": L0["Wq"].T, "wkT": L0["Wk"].T, "wvT": L0["Wv"].T, "woT": L0["Wo"].T,
        "bq": L0["bq"].reshape(PAIRS, P).T, "bk": L0["bk"].reshape(PAIRS, P).T,
        "bv": L0["bv"], "bo": L0["bo"], "gamma": L0["gamma"], "beta": L0["beta"],
        "w": W.transpose(1, 0, 2), "a1": a[:, :D], "a2": a[:, D:],
    }
    nc = bacc.Bacc("TRN2", target_bir_lowering=False, num_devices=1, dynamic_dma_scratch_size=1024)
    arrays, args = {}, []
    for name, v in laid_out.items():
        arrays[name] = np.ascontiguousarray(v)
        args.append(nc.dram_tensor(name, v.shape, mybir.dt.from_np(v.dtype), kind="ExternalInput").ap())
    args.append(nc.dram_tensor("out", (NB, N, F), F32, kind="ExternalOutput").ap())
    build(nc, *args)
    r = run_bass_kernel_spmd(nc, [arrays], core_ids=[0])
    return r.results[0]["out"]
```
